# Optimizing a Trainium2 kernel written in Bass

```python
import numpy as np
import jax
import jax.numpy as jnp

def _softmax(x, axis=-1):
    return jax.nn.softmax(x, axis=axis)

def _gelu(x):
    return jax.nn.gelu(x, approximate=True)

def _silu(x):
    return jax.nn.silu(x)

def _sigmoid(x):
    return jax.nn.sigmoid(x)

def _layernorm(x, axis=-1, eps=1e-05):
    m = jnp.mean(x, axis=axis, keepdims=True)
    v = jnp.var(x, axis=axis, keepdims=True)
    return (x - m) / jnp.sqrt(v + eps)

def _scatter_add(tgt, idx, src, axis=0):
    return tgt.at[idx].add(src)

def _segment_sum(src, seg, n):
    return jax.ops.segment_sum(src, seg, n)
kernel_name = 'mk_flamingo_gated_d2_seqx_r4_491851'

def setup_inputs(seed: int=0):
    np.random.seed(seed)
    _w = jnp.asarray

    def _rec_inputs():
        import jax
        import jax.numpy as jnp
        _rk = jax.random.key(seed)
        x = -0.0003929 + 0.9999 * jax.random.normal(jax.random.fold_in(_rk, 1), (32, 112, 256), jnp.float32)
        _lenS = 112 - jax.random.randint(jax.random.fold_in(_rk, 7), (32,), 0, max(1, 112 // 4) + 1, jnp.int32)
        _lenS2 = 375 - jax.random.randint(jax.random.fold_in(_rk, 8), (32,), 0, max(1, 375 // 4) + 1, jnp.int32)
        _ctx_2048P = jax.random.normal(jax.random.fold_in(_rk, 11), (32, 16, 512), jnp.float32)
        _ctx_2048c = jax.random.dirichlet(jax.random.fold_in(_rk, 511), 0.3 * jnp.ones((16,), jnp.float32), (32, 375))
        _ctx_2048t = jnp.einsum('bsk,bkd->bsd', _ctx_2048c, _ctx_2048P)
        _ctx_2048t = _ctx_2048t * jax.lax.rsqrt(jnp.mean(jnp.square(_ctx_2048t)) + 1e-12) * 0.953939
        ctx_2048 = 4.13588e-05 + 0.999923 * (_ctx_2048t + 0.3 * jax.random.normal(jax.random.fold_in(_rk, 611), (32, 375, 512), jnp.float32))
        _validS = jnp.arange(112)[None, :] < _lenS[:, None]
        _validS2 = jnp.arange(375)[None, :] < _lenS2[:, None]
        _causal = jnp.tril(jnp.ones((112, 112), dtype=bool))
        mask_BxS2_if0 = jnp.where(jnp.ones((32, 375), dtype=bool), 4, 0).astype(jnp.int32)
        _g = jax.random.normal(jax.random.fold_in(_rk, 9001), (2, 2), jnp.float32)
        _g = jnp.sign(_g) * jnp.maximum(jnp.abs(_g), 1.0) + (_g == 0) * 1.0
        g_xattn = _g[0]
        g_ffn = _g[1]
        return (x, ctx_2048, mask_BxS2_if0, g_xattn, g_ffn)
    x, ctx_2048, mask_BxS2_if0, g_xattn, g_ffn = _rec_inputs()

    def _L0_xattn_setup():
        import jax, jax.numpy as jnp
        import numpy as np
        B, L, P = (4, 1024, 256)
        D_MODEL = 256
        D_GLOBAL = 512
        HEADDIM = 32
        EPSILON = 0.001
        RMS_EPS = 1e-05

        def rmsnorm(x, g, eps=RMS_EPS):
            var = jnp.mean(jnp.square(x), axis=-1, keepdims=True)
            return x * jax.lax.rsqrt(var + eps) * g

        def _hnet_depool(h, h_patch_full, patch_lens):
            h_patch = h_patch_full[..., :D_MODEL]
            bsz, plen = (h_patch.shape[0], h_patch.shape[1])
            seqlen = h.shape[1]
            logp = jnp.full((bsz, plen), -EPSILON, dtype=jnp.float32)
            bidx = jnp.cumsum(patch_lens, axis=1) - 1
            boundary_mask = jnp.zeros((bsz, seqlen), dtype=jnp.int32)
            boundary_mask = boundary_mask.at[jnp.arange(bsz)[:, None], bidx].set(1)
            dt = (-jnp.log(-jnp.expm1(logp))).astype(h_patch.dtype)
            x = h_patch / dt[..., None]
            n_heads = D_MODEL // HEADDIM
            A = -jnp.ones((n_heads,), dtype=jnp.float32)
            bcoef = jnp.exp(logp).astype(h_patch.dtype)
            x4 = x.reshape(bsz, plen, n_heads, HEADDIM)
            a = jnp.exp(dt[:, :, None] * A[None, None, :])
            u = (dt * bcoef)[:, :, None, None] * x4
            a_b = jnp.broadcast_to(a[..., None], u.shape)

            def comb(lft, rgt):
                aL, uL = lft
                aR, uR = rgt
                return (aL * aR, uL * aR + uR)
            _, s = jax.lax.associative_scan(comb, (a_b, u), axis=1)
            depool = s.reshape(bsz, plen, D_MODEL)
            plug = jnp.clip(jnp.cumsum(boundary_mask, axis=1) - 1, 0, plen - 1)
            depool_out = depool[jnp.arange(bsz)[:, None], plug]
            return depool_out + h
        key = jax.random.key(seed)
        k1, k2, k3, k4 = jax.random.split(key, 4)
        embeds = jax.random.normal(k1, (B, L, D_MODEL), dtype=jnp.float32)
        patch_embeds = jax.random.normal(k2, (B, P, D_GLOBAL), dtype=jnp.float32)
        patch_lens = jnp.full((B, P), L // P, dtype=jnp.int64)
        W_in = jax.random.normal(k3, (D_MODEL, D_MODEL), dtype=jnp.float32) * 0.02
        b_in = jnp.zeros((D_MODEL,), dtype=jnp.float32)
        g_res = jnp.ones((D_MODEL,), dtype=jnp.float32)
        g_init = jnp.ones((D_GLOBAL,), dtype=jnp.float32)
        return {'embeds': embeds, 'patch_embeds': patch_embeds, 'patch_lens': patch_lens, 'W_in': W_in, 'b_in': b_in, 'g_res': g_res, 'g_init': g_init}
    _L0_xattn_all = _L0_xattn_setup()
    _L0_xattn_in = {k: v for k, v in _L0_xattn_all.items() if k in ('W_in', 'b_in', 'g_res', 'g_init')}
    del _L0_xattn_all

    def _L0_ffn_setup():
        import jax, jax.numpy as jnp
        import numpy as np
        B, S, H, F, E = (8, 512, 256, 1024, 8)
        INIT_LAMBDA = 0.2
        key = jax.random.key(seed)
        ks = jax.random.split(key, 12)
        std = 0.02
        return {'hidden_states': jax.random.normal(ks[0], (B, S, H), jnp.float32), 'gate_w1': jax.random.normal(ks[1], (H, H), jnp.float32) * 0.01, 'gate_b1': jnp.zeros((H,), jnp.float32), 'gate_w2': jax.random.normal(ks[2], (E, H), jnp.float32) * 0.01, 'gate_b2': jnp.full((E,), INIT_LAMBDA, jnp.float32), 'W1': jax.random.normal(ks[3], (F, H), jnp.float32) * std, 'b1': jax.random.normal(ks[4], (F,), jnp.float32) * std, 'W2': jax.random.normal(ks[5], (H, F), jnp.float32) * std, 'b2': jax.random.normal(ks[6], (H,), jnp.float32) * std, 'TW1': jax.random.normal(ks[7], (E, F, H), jnp.float32) * std, 'Tb1': jax.random.normal(ks[8], (E, F), jnp.float32) * std, 'TW2': jax.random.normal(ks[9], (E, H, F), jnp.float32) * std, 'Tb2': jax.random.normal(ks[10], (E, H), jnp.float32) * std}
    _L0_ffn_all = _L0_ffn_setup()
    _L0_ffn_in = {k: v for k, v in _L0_ffn_all.items() if k in ('gate_w1', 'gate_b1', 'gate_w2', 'gate_b2', 'W1', 'b1', 'W2', 'b2', 'TW1', 'Tb1', 'TW2', 'Tb2')}
    del _L0_ffn_all

    def _L1_xattn_setup():
        import jax, jax.numpy as jnp
        import numpy as np
        NUM_HEADS = 16
        key = jax.random.key(seed)
        ks = jax.random.split(key, 5)
        dim = 256
        B, N, N_c = (4, 256, 64)
        x = jax.random.normal(ks[0], (B, N, dim), dtype=jnp.float32)
        context = jax.random.normal(ks[1], (B, N_c, 2 * dim), dtype=jnp.float32)
        w_qkv = jax.random.normal(ks[2], (3 * dim, dim), dtype=jnp.float32) * 0.02
        w_proj = jax.random.normal(ks[3], (dim, dim), dtype=jnp.float32) * 0.02
        b_proj = jax.random.normal(ks[4], (dim,), dtype=jnp.float32) * 0.02
        return {'x': x, 'context': context, 'w_qkv': w_qkv, 'w_proj': w_proj, 'b_proj': b_proj}
    _L1_xattn_all = _L1_xattn_setup()
    _L1_xattn_in = {k: v for k, v in _L1_xattn_all.items() if k in ('w_qkv', 'w_proj', 'b_proj')}
    del _L1_xattn_all

    def _L1_ffn_setup():
        import jax, jax.numpy as jnp
        import numpy as np
        NUM_COLUMNS = 16
        INPUT_DIM = 256
        NUM_NEURONS = 64
        SPARSITY = 0.05
        B, S = (4, 512)

        def _l2norm(v, axis=-1, eps=1e-12):
            n = jnp.sqrt(jnp.sum(v * v, axis=axis, keepdims=True))
            return v / jnp.maximum(n, eps)
        key = jax.random.key(seed)
        ks = jax.random.split(key, 12)
        D, C, N = (INPUT_DIM, NUM_COLUMNS, NUM_NEURONS)
        inp = {'x': jax.random.normal(ks[0], (B, S, D), dtype=jnp.float32), 'col_emb': jax.random.normal(ks[1], (C, D), dtype=jnp.float32) * 0.02, 'gate_w1': jax.random.normal(ks[2], (D, D // 2), dtype=jnp.float32) / np.sqrt(D), 'gate_b1': jnp.zeros((D // 2,), dtype=jnp.float32), 'gate_w2': jax.random.normal(ks[3], (D // 2, C), dtype=jnp.float32) / np.sqrt(D // 2), 'gate_b2': jnp.zeros((C,), dtype=jnp.float32), 'W_cols': jax.random.normal(ks[4], (C, D, N), dtype=jnp.float32) / np.sqrt(D), 'b_cols': jnp.zeros((C, N), dtype=jnp.float32), 'proj_w': jax.random.normal(ks[5], (C * N, D), dtype=jnp.float32) / np.sqrt(C * N), 'proj_b': jnp.zeros((D,), dtype=jnp.float32), 'ln_g': jnp.ones((D,), dtype=jnp.float32), 'ln_b': jnp.zeros((D,), dtype=jnp.float32)}
        return inp
    _L1_ffn_all = _L1_ffn_setup()
    _L1_ffn_in = {k: v for k, v in _L1_ffn_all.items() if k in ('col_emb', 'gate_w1', 'gate_b1', 'gate_w2', 'gate_b2', 'W_cols', 'b_cols', 'proj_w', 'proj_b', 'ln_g', 'ln_b')}
    del _L1_ffn_all
    return {'x': x, 'ctx_2048': ctx_2048, 'mask_BxS2_if0': mask_BxS2_if0, 'g_xattn': g_xattn, 'g_ffn': g_ffn, 'L0_xattn_W_in': _L0_xattn_in['W_in'], 'L0_xattn_b_in': _L0_xattn_in['b_in'], 'L0_xattn_g_res': _L0_xattn_in['g_res'], 'L0_xattn_g_init': _L0_xattn_in['g_init'], 'L0_ffn_gate_w1': _L0_ffn_in['gate_w1'], 'L0_ffn_gate_b1': _L0_ffn_in['gate_b1'], 'L0_ffn_gate_w2': _L0_ffn_in['gate_w2'], 'L0_ffn_gate_b2': _L0_ffn_in['gate_b2'], 'L0_ffn_W1': _L0_ffn_in['W1'], 'L0_ffn_b1': _L0_ffn_in['b1'], 'L0_ffn_W2': _L0_ffn_in['W2'], 'L0_ffn_b2': _L0_ffn_in['b2'], 'L0_ffn_TW1': _L0_ffn_in['TW1'], 'L0_ffn_Tb1': _L0_ffn_in['Tb1'], 'L0_ffn_TW2': _L0_ffn_in['TW2'], 'L0_ffn_Tb2': _L0_ffn_in['Tb2'], 'L1_xattn_w_qkv': _L1_xattn_in['w_qkv'], 'L1_xattn_w_proj': _L1_xattn_in['w_proj'], 'L1_xattn_b_proj': _L1_xattn_in['b_proj'], 'L1_ffn_col_emb': _L1_ffn_in['col_emb'], 'L1_ffn_gate_w1': _L1_ffn_in['gate_w1'], 'L1_ffn_gate_b1': _L1_ffn_in['gate_b1'], 'L1_ffn_gate_w2': _L1_ffn_in['gate_w2'], 'L1_ffn_gate_b2': _L1_ffn_in['gate_b2'], 'L1_ffn_W_cols': _L1_ffn_in['W_cols'], 'L1_ffn_b_cols': _L1_ffn_in['b_cols'], 'L1_ffn_proj_w': _L1_ffn_in['proj_w'], 'L1_ffn_proj_b': _L1_ffn_in['proj_b'], 'L1_ffn_ln_g': _L1_ffn_in['ln_g'], 'L1_ffn_ln_b': _L1_ffn_in['ln_b']}

def reference(x, ctx_2048, mask_BxS2_if0, g_xattn, g_ffn, L0_xattn_W_in, L0_xattn_b_in, L0_xattn_g_res, L0_xattn_g_init, L0_ffn_gate_w1, L0_ffn_gate_b1, L0_ffn_gate_w2, L0_ffn_gate_b2, L0_ffn_W1, L0_ffn_b1, L0_ffn_W2, L0_ffn_b2, L0_ffn_TW1, L0_ffn_Tb1, L0_ffn_TW2, L0_ffn_Tb2, L1_xattn_w_qkv, L1_xattn_w_proj, L1_xattn_b_proj, L1_ffn_col_emb, L1_ffn_gate_w1, L1_ffn_gate_b1, L1_ffn_gate_w2, L1_ffn_gate_b2, L1_ffn_W_cols, L1_ffn_b_cols, L1_ffn_proj_w, L1_ffn_proj_b, L1_ffn_ln_g, L1_ffn_ln_b):
    import jax
    import jax.numpy as jnp

    def _L0_xattn_ref(embeds, patch_embeds, patch_lens, W_in, b_in, g_res, g_init):
        import jax, jax.numpy as jnp
        import numpy as np
        B, L, P = (4, 1024, 256)
        D_MODEL = 256
        D_GLOBAL = 512
        HEADDIM = 32
        EPSILON = 0.001
        RMS_EPS = 1e-05

        def rmsnorm(x, g, eps=RMS_EPS):
            var = jnp.mean(jnp.square(x), axis=-1, keepdims=True)
            return x * jax.lax.rsqrt(var + eps) * g

        def _hnet_depool(h, h_patch_full, patch_lens):
            h_patch = h_patch_full[..., :D_MODEL]
            bsz, plen = (h_patch.shape[0], h_patch.shape[1])
            seqlen = h.shape[1]
            logp = jnp.full((bsz, plen), -EPSILON, dtype=jnp.float32)
            bidx = jnp.cumsum(patch_lens, axis=1) - 1
            boundary_mask = jnp.zeros((bsz, seqlen), dtype=jnp.int32)
            boundary_mask = boundary_mask.at[jnp.arange(bsz)[:, None], bidx].set(1)
            dt = (-jnp.log(-jnp.expm1(logp))).astype(h_patch.dtype)
            x = h_patch / dt[..., None]
            n_heads = D_MODEL // HEADDIM
            A = -jnp.ones((n_heads,), dtype=jnp.float32)
            bcoef = jnp.exp(logp).astype(h_patch.dtype)
            x4 = x.reshape(bsz, plen, n_heads, HEADDIM)
            a = jnp.exp(dt[:, :, None] * A[None, None, :])
            u = (dt * bcoef)[:, :, None, None] * x4
            a_b = jnp.broadcast_to(a[..., None], u.shape)

            def comb(lft, rgt):
                aL, uL = lft
                aR, uR = rgt
                return (aL * aR, uL * aR + uR)
            _, s = jax.lax.associative_scan(comb, (a_b, u), axis=1)
            depool = s.reshape(bsz, plen, D_MODEL)
            plug = jnp.clip(jnp.cumsum(boundary_mask, axis=1) - 1, 0, plen - 1)
            depool_out = depool[jnp.arange(bsz)[:, None], plug]
            return depool_out + h
        h = rmsnorm(embeds, g_res)
        h = jnp.einsum('bld,ed->ble', h, W_in) + b_in
        h_patch = rmsnorm(patch_embeds, g_init)
        return _hnet_depool(h, h_patch, patch_lens)

    def _L0_ffn_ref(hidden_states, gate_w1, gate_b1, gate_w2, gate_b2, W1, b1, W2, b2, TW1, Tb1, TW2, Tb2):
        import jax, jax.numpy as jnp
        import numpy as np
        B, S, H, F, E = (8, 512, 256, 1024, 8)
        INIT_LAMBDA = 0.2
        x = hidden_states
        h = jax.nn.relu(jnp.einsum('bsh,oh->bso', x, gate_w1) + gate_b1)
        g = jnp.einsum('bso,eo->bse', h, gate_w2) + gate_b2
        g = g.mean(axis=1)
        mW1 = W1 + jnp.einsum('be,efh->bfh', g, TW1)
        mb1 = b1 + g @ Tb1
        mW2 = W2 + jnp.einsum('be,ehf->bhf', g, TW2)
        mb2 = b2 + g @ Tb2
        u = jax.nn.gelu(jnp.einsum('bsh,bfh->bsf', x, mW1) + mb1[:, None, :])
        out = jnp.einsum('bsf,bhf->bsh', u, mW2) + mb2[:, None, :]
        return out

    def _L1_xattn_ref(x, context, w_qkv, w_proj, b_proj):
        import jax, jax.numpy as jnp
        import numpy as np
        NUM_HEADS = 16
        B, N, C = x.shape
        H = NUM_HEADS
        D = C // H
        scale = D ** (-0.5)
        qkv = (x @ w_qkv.T).reshape(B, N, 3, H, D).transpose(2, 0, 3, 1, 4)
        q, k, v = (qkv[0], qkv[1], qkv[2])
        N_c = context.shape[1]
        kv = context.reshape(B, N_c, 2, H, D).transpose(2, 0, 3, 1, 4)
        extra_k, extra_v = (kv[0], kv[1])
        k = jnp.concatenate([extra_k, k], axis=2)
        v = jnp.concatenate([extra_v, v], axis=2)
        dtype = q.dtype
        attn = jnp.einsum('bhnd,bhmd->bhnm', q * scale, k).astype(jnp.float32)
        attn = jax.nn.softmax(attn, axis=-1).astype(dtype)
        out = jnp.einsum('bhnm,bhmd->bhnd', attn, v)
        out = out.transpose(0, 2, 1, 3).reshape(B, N, C)
        return out @ w_proj.T + b_proj

    def _L1_ffn_ref(x, col_emb, gate_w1, gate_b1, gate_w2, gate_b2, W_cols, b_cols, proj_w, proj_b, ln_g, ln_b):
        import jax, jax.numpy as jnp
        import numpy as np
        NUM_COLUMNS = 16
        INPUT_DIM = 256
        NUM_NEURONS = 64
        SPARSITY = 0.05
        B, S = (4, 512)

        def _l2norm(v, axis=-1, eps=1e-12):
            n = jnp.sqrt(jnp.sum(v * v, axis=axis, keepdims=True))
            return v / jnp.maximum(n, eps)
        Bq, Sq, D = x.shape
        C = col_emb.shape[0]
        similarity = jnp.einsum('bsd,cd->bsc', _l2norm(x), _l2norm(col_emb))
        h = jax.nn.gelu(x @ gate_w1 + gate_b1, approximate=False)
        gate_values = jax.nn.sigmoid(h @ gate_w2 + gate_b2)
        logits = similarity + gate_values
        k = max(1, int(C * SPARSITY))
        _, top_idx = jax.lax.top_k(logits, k)
        mask = jnp.sum(jax.nn.one_hot(top_idx, C, dtype=logits.dtype), axis=-2)
        weights = mask * jax.nn.softmax(logits, axis=-1)
        cols = jax.nn.gelu(jnp.einsum('bsd,cdn->bscn', x, W_cols) + b_cols, approximate=False)
        cols = cols * weights[..., None]
        combined = cols.reshape(Bq, Sq, -1)
        y = combined @ proj_w + proj_b + x
        mu = jnp.mean(y, axis=-1, keepdims=True)
        var = jnp.mean((y - mu) ** 2, axis=-1, keepdims=True)
        out = (y - mu) * jax.lax.rsqrt(var + 1e-05) * ln_g + ln_b
        return out
    x = x + jnp.tanh(g_xattn[0]) * _L0_xattn_ref(_layernorm(x, axis=-1), ctx_2048, mask_BxS2_if0, L0_xattn_W_in, L0_xattn_b_in, L0_xattn_g_res, L0_xattn_g_init)
    x = x + jnp.tanh(g_ffn[0]) * _L0_ffn_ref(_layernorm(x, axis=-1), L0_ffn_gate_w1, L0_ffn_gate_b1, L0_ffn_gate_w2, L0_ffn_gate_b2, L0_ffn_W1, L0_ffn_b1, L0_ffn_W2, L0_ffn_b2, L0_ffn_TW1, L0_ffn_Tb1, L0_ffn_TW2, L0_ffn_Tb2)
    x = x + jnp.tanh(g_xattn[1]) * _L1_xattn_ref(_layernorm(x, axis=-1), ctx_2048, L1_xattn_w_qkv, L1_xattn_w_proj, L1_xattn_b_proj)
    x = x + jnp.tanh(g_ffn[1]) * _L1_ffn_ref(_layernorm(x, axis=-1), L1_ffn_col_emb, L1_ffn_gate_w1, L1_ffn_gate_b1, L1_ffn_gate_w2, L1_ffn_gate_b2, L1_ffn_W_cols, L1_ffn_b_cols, L1_ffn_proj_w, L1_ffn_proj_b, L1_ffn_ln_g, L1_ffn_ln_b)
    return x

_drawn_inputs = setup_inputs


def setup_inputs(seed=0):
    import zlib

    import numpy as np

    out = dict(_drawn_inputs(seed))
    spreads = {'g_ffn': (-1.0, 0.2),
     'L0_xattn_b_in': (0.0, 0.1),
     'L0_xattn_g_res': (1.0, 0.2),
     'L0_xattn_g_init': (1.0, 0.2),
     'L0_ffn_gate_b1': (0.0, 0.8),
     'L0_ffn_gate_b2': (0.20000000298023224, 0.6),
     'L1_ffn_gate_b1': (0.0, 0.8),
     'L1_ffn_gate_b2': (0.0, 0.699),
     'L1_ffn_b_cols': (0.0, 0.8),
     'L1_ffn_proj_b': (0.0, 0.1),
     'L1_ffn_ln_g': (1.0, 0.2),
     'L1_ffn_ln_b': (0.0, 0.1)}
    factors = {'L0_ffn_gate_w1': 8.0,
     'L0_ffn_gate_w2': 8.0,
     'L0_ffn_b1': 8.0,
     'L0_ffn_b2': 4.68,
     'L0_ffn_Tb1': 8.0,
     'L0_ffn_Tb2': 7.861,
     'L1_xattn_w_qkv': 4.649,
     'L1_xattn_b_proj': 3.992,
     'L1_ffn_col_emb': 4.002,
     'L1_ffn_gate_w1': 3.163,
     'L1_ffn_gate_w2': 2.897,
     'L1_ffn_W_cols': 3.102,
     'L1_ffn_proj_w': 2.805}
    for name, (base, spread) in spreads.items():
        noise = np.random.default_rng([zlib.crc32(name.encode()), seed]).standard_normal(out[name].shape)
        drawn = base * np.exp(spread * noise) if base else spread * noise
        out[name] = jnp.asarray(drawn.astype(out[name].dtype))
    for name, factor in factors.items():
        out[name] = (out[name] * factor).astype(out[name].dtype)
    return out
```

```python
from contextlib import ExitStack

import concourse.bass as bass
from concourse import mybir
import numpy as np

ALU = mybir.AluOpType
ACT = mybir.ActivationFunctionType
AX = mybir.AxisListType
F32 = mybir.dt.float32
BF16 = mybir.dt.bfloat16
I32 = mybir.dt.int32

B, T, D = 32, 112, 256
S2, DC = 375, 512
P = 128
KD = D // P
GB = 4
NG = B // GB
GT = GB * T
CHUNK = 125
NC = S2 // CHUNK + 1
KPAD = NC * CHUNK
NKEY = S2 + T
EPS = 1e-5
F, E = 1024, 8
ER = P // E
FC = F // P
H, DH, SLOT = 16, 16, 32
HS = P // SLOT
NT = H // HS
C4, N4 = 16, 64
F4 = C4 * N4
J4 = F4 // P
DEPOOL_EPS = 0.001
CREDIT = 4


def nth(n):
    return n + (1 + CREDIT)


class Chain:

    def __init__(self, eng, sem):
        self.eng, self.sem, self.base, self.k = eng, sem, 0, 0

    def link(self, ins):
        self.k += 1
        ins.then_inc(self.sem, 1)
        self.eng.wait_ge(self.sem, self.base + self.k)

    def loop(self, count, per, body):
        start = self.base + self.k
        with self.eng.Fori(0, count) as i:
            self.base, self.k = start + i * per, 0
            body(i)
            assert self.k == per, (self.k, per)
        self.base, self.k = start + count * per, 0


def alone(w, eng):
    eng.sem_inc(w.carried, 1)


def statistics(nc, w, chain, stats, mean_var, x):
    alone(w, chain.eng)
    chain.link(nc.vector.bn_stats(stats, x))
    alone(w, chain.eng)
    return nc.vector.bn_aggr(mean_var, stats)


def inverse_root(nc, chain, out, root, v, tmp):
    chain.link(nc.vector.reciprocal(out, root))
    chain.link(nc.vector.tensor_tensor(tmp, out, out, ALU.mult))
    chain.link(nc.vector.tensor_tensor(tmp, tmp, v, ALU.mult))
    chain.link(nc.vector.tensor_scalar(tmp, tmp, -0.5, 1.5, ALU.mult, ALU.add))
    return nc.vector.tensor_tensor(out, out, tmp, ALU.mult)


def normalised(nc, w, out, b):
    return nc.vector.tensor_scalar(out, w.x_res[:, b, :], w.mean_var[:, b, 0:1], w.rstd[:, b, :],
                                   ALU.subtract, ALU.mult)


def row_statistics(nc, chain, w):
    with w.nc.sbuf_tensor(f"stats{len(w.stat_uses)}", [T, B, 6], F32) as stats:
        w.stat_uses.append(1)
        for g in range(NG):
            for r in range(GB):
                last = nc.vector.bn_stats(stats[:, g * GB + r, :], w.x_res[:, g * GB + r, :])
            chain.link(last)
            for r in range(GB):
                last = nc.vector.bn_aggr(w.mean_var[:, g * GB + r, :], stats[:, g * GB + r, :])
        chain.link(last)


def build(nc, a, out):
    ctx = ExitStack()
    with ctx:
        world = World(nc, a, out, ctx)
        setup(world)
        stage1(world)
        stage2(world)
        stage3(world)
        stage4(world)


class World:

    def __init__(self, nc, a, out, ctx):
        self.nc, self.a, self.out, self.ctx = nc, a, out, ctx
        sb = lambda n, s, d=F32: ctx.enter_context(nc.sbuf_tensor(n, s, d))
        self.x_res = sb("x_res", [T, B, D])
        self.mean_var = sb("mean_var", [T, B, 2])
        self.rstd = sb("rstd", [T, B, 1])
        self.ident = sb("ident", [P, P])
        self.gates = sb("gates", [P, 4])
        self.x_in = [self.sem(f"x_in{g}") for g in range(NG)]
        self.banks = ctx.enter_context(nc.psum_tensor("banks", [P, 8, 512], F32))
        self.stat_uses = []
        self.carried = self.sem("carried")

    def sem(self, name):
        return self.ctx.enter_context(self.nc.semaphore(name))

    def bank(self, n, parts=P, cols=512):
        return self.banks[0:parts, n, 0:cols]


def setup(w):
    nc, a = w.nc, w.a
    consts_in, graw_in = w.sem("consts_in"), w.sem("graw_in")
    with nc.sbuf_tensor("gates_raw", [P, 4], F32) as gates_raw, nc.Block() as block:
        @block.sync
        def _(sp):
            for n, g in enumerate((a["g_xattn"], a["g_ffn"])):
                sp.dma_start(gates_raw[:, 2 * n:2 * n + 2], g.partition_broadcast(P)).then_inc(graw_in, 16)
            sp.dma_start(w.ident[:], a["ident"]).then_inc(consts_in, 16)
            for g in range(NG):
                sp.dma_start(w.x_res[:, g * GB:(g + 1) * GB, :],
                             a["x"][g * GB:(g + 1) * GB].rearrange("b t d -> t b d")).then_inc(w.x_in[g], 16)
            sp.wait_ge(consts_in, 16)

        @block.scalar
        def _(act):
            act.wait_ge(graw_in, 32)
            nc.scalar.activation(w.gates[:], gates_raw[:], ACT.Tanh)


def stage1(w):
    nc, a = w.nc, w.a
    dt = float(-np.log(-np.expm1(-DEPOOL_EPS)))
    bcoef = float(np.exp(-DEPOOL_EPS))
    NQ = S2 // CHUNK
    U = 4
    with ExitStack() as ctx:
        sb = lambda n, s, d=F32: ctx.enter_context(nc.sbuf_tensor(n, s, d))
        sem = w.sem
        w_in = sb("s1_w_in", [P, KD, D])
        g_res = sb("s1_g_res", [P, KD])
        g_init = sb("s1_g_init", [T, D])
        mask_i = sb("s1_mask_i", [B, S2], I32)
        mask_f = sb("s1_mask_f", [B, S2])
        zero = sb("s1_zero", [B, S2])
        cum = sb("s1_cum", [B, S2])
        idx = sb("s1_idx", [B, S2])
        wrap = sb("s1_wrap", [B, S2])
        idx_t = sb("s1_idx_t", [CHUNK, NQ * B])
        iota = sb("s1_iota", [P, T + 1])
        ones16 = sb("s1_ones16", [CHUNK, T], BF16)
        hit = sb("s1_hit", [CHUNK, NQ * B, T], BF16)
        mark = sb("s1_mark", [T, B * T])
        keep = sb("s1_keep", [T, B, T])
        plug = sb("s1_plug", [T, B * T])
        pos = sb("s1_pos", [T, B * T])
        expo = sb("s1_expo", [T, B * T])
        ctx_rows = sb("s1_ctx_rows", [T, U, DC])
        ctx_u = sb("s1_ctx_u", [T, B, D])
        ms = sb("s1_ms", [T, 2, B])
        root = sb("s1_root", [T, 2, B])
        inv = sb("s1_inv", [T, 2, B, 1])
        tmp = sb("s1_tmp", [T, 2, B])
        u = sb("s1_u", [P, 2, D])
        m_scan = sb("s1_m_scan", [P, 2, T])
        xn = sb("s1_xn", [T, 2, D])
        x_t = sb("s1_x_t", [P, 2, KD, T])
        stats = sb("s1_stats", [T, B, 6])
        x_mv = sb("s1_x_mv", [T, U, 2])

        loads, mask_in, bias_in = sem("s1_loads"), sem("s1_mask_in"), sem("s1_bias_in")
        ctx_in = [sem(f"s1_ctx_in{u_}") for u_ in range(U)]
        cleared, idx_done, idx_tr, hit_done, counted = (sem("s1_" + n) for n in (
            "cleared", "idx_done", "idx_tr", "hit_done", "counted"))
        prep, expo_done = sem("s1_prep"), sem("s1_expo_done")
        xn_done, x_tr, x_t_done, m_done = (sem("s1_" + n) for n in ("xn_done", "x_tr", "x_t_done", "m_done"))
        squared, ms_done, root_done, u_done, y_done, x_done, chain_s = (sem("s1_" + n) for n in (
            "squared", "ms_done", "root_done", "u_done", "y_done", "x_done", "chain"))
        ctx_u_in = [sem(f"s1_ctx_u_in{g}") for g in range(NG)]

        with nc.Block() as block:
            @block.sync
            def _(sp):
                sp.dma_start(mask_i[:], a["mask"]).then_inc(mask_in, 16)
                for dst, src in ((iota[:], a["iota"]), (w_in[:], a["w_in_t"]), (g_res[:], a["g_res_c"]),
                                 (g_init[:], a["g_init_row"].partition_broadcast(T))):
                    sp.dma_start(dst, src).then_inc(loads, 16)
                sp.wait_ge(cleared, 1)
                for k in range(2):
                    sp.dma_start(u[T:T + 1, k, :], a["b_in_row"]).then_inc(bias_in, 16)
                with sp.Fori(0, B // U) as i:
                    for r in range(U):
                        b = U * i + r
                        sp.wait_ge(squared, nth(b - U))
                        sp.dma_start(ctx_rows[:, r, :], a["ctx"][b, 0:T, :]).then_inc(ctx_in[r], 16)
                for g in range(NG):
                    sp.dma_start(ctx_u[:, g * GB:(g + 1) * GB, :],
                                 a["ctx"][g * GB:(g + 1) * GB, 0:T, 0:D].rearrange("b t d -> t b d")).then_inc(ctx_u_in[g], 16)

            @block.vector
            def _(dve):
                chain = Chain(dve, chain_s)
                for s in (xn_done, u_done, x_done):
                    dve.sem_inc(s, CREDIT)
                nc.vector.memset(u[:], 0.0).then_inc(cleared, 1)
                nc.vector.memset(zero[:], 0.0)
                nc.vector.memset(ones16[:], 1.0)
                nc.vector.memset(keep[:], 1.0)
                chain.link(nc.vector.memset(m_scan[:], 1.0))
                chain.link(nc.vector.memset(keep[:, :, 0:1], 0.0))
                for g in range(NG):
                    dve.wait_ge(w.x_in[g], 16)
                    for r in range(GB):
                        last = nc.vector.bn_stats(stats[:, g * GB + r, :], w.x_res[:, g * GB + r, :])
                    chain.link(last)
                    for r in range(GB):
                        last = nc.vector.bn_aggr(w.mean_var[:, g * GB + r, :], stats[:, g * GB + r, :])
                chain.link(last)
                dve.wait_ge(squared, nth(B - 1))
                chain.link(nc.vector.tensor_scalar(ms[:, 0, :], ms[:, 0, :], 1.0 / DC, EPS, ALU.mult, ALU.add))
                nc.vector.tensor_scalar(ms[:, 1, :], w.mean_var[:, :, 1], 1 + EPS, EPS * EPS, ALU.mult,
                                        ALU.add).then_inc(ms_done, 1)
                dve.wait_ge(mask_in, 16)
                chain.link(nc.vector.tensor_copy(mask_f[:], mask_i[:]))
                chain.link(nc.vector.tensor_tensor_scan(cum[:], mask_f[:], zero[:], 0.0, ALU.add, ALU.add))
                nc.vector.tensor_scalar(wrap[:], cum[:], 1.0, float(T), ALU.is_lt, ALU.mult)
                chain.link(nc.vector.tensor_scalar(idx[:], cum[:], -1.0, None, ALU.add))
                nc.vector.tensor_tensor(idx[:], idx[:], wrap[:], ALU.add).then_inc(idx_done, 1)
                dve.wait_ge(loads, 16 * 4)
                for kk in range(KD):
                    chain.link(nc.vector.tensor_scalar(w_in[:, kk, :], w_in[:, kk, :], g_res[:, kk:kk + 1],
                                                       w.gates[:, 0:1], ALU.mult, ALU.mult))
                chain.link(nc.vector.tensor_scalar(g_init[:], g_init[:], w.gates[0:T, 0:1],
                                                   bcoef, ALU.mult, ALU.mult))
                dve.wait_ge(bias_in, 32)
                chain.link(nc.vector.tensor_scalar(u[96:T + 1, :, :], u[96:T + 1, :, :],
                                                   w.gates[96:T + 1, 0:1], None, ALU.mult))
                dve.wait_ge(idx_tr, 1)
                chain.link(nc.vector.tensor_copy(idx_t[:], w.bank(0, CHUNK, NQ * B)))
                nc.vector.tensor_tensor(
                    hit[:], iota[0:CHUNK, 0:T].unsqueeze(1).broadcast_to([CHUNK, NQ * B, T]),
                    idx_t[:].unsqueeze(2).broadcast_to([CHUNK, NQ * B, T]), ALU.is_equal).then_inc(hit_done, 1)
                dve.wait_ge(counted, 1)
                for g in range(NG):
                    last = nc.vector.tensor_scalar(mark[:, g * GT:(g + 1) * GT], w.bank(g, T, GT), 1.0, None, ALU.min)
                chain.link(last)
                chain.link(nc.vector.tensor_tensor_scan(plug[:], keep[:].rearrange("p b t -> p (b t)"), mark[:],
                                                        0.0, ALU.mult, ALU.add))
                chain.link(nc.vector.tensor_scalar(pos[:], plug[:], -1.0, 0.0, ALU.add, ALU.max))
                nc.vector.tensor_scalar(plug[:], pos[:], iota[0:T, T:T + 1], -dt, ALU.subtract, ALU.mult)
                chain.link(nc.vector.tensor_scalar(pos[:], pos[:], iota[0:T, T:T + 1], 1000.0, ALU.subtract, ALU.mult))
                nc.vector.tensor_tensor(expo[:], plug[:], pos[:], ALU.min).then_inc(expo_done, 1)
                dve.wait_ge(root_done, 1)
                chain.link(inverse_root(nc, chain, inv[:, :, :, 0], root[:], ms[:], tmp[:]))
                for g in range(NG):
                    dve.wait_ge(ctx_u_in[g], 16)

                def front(b, r):
                    dve.wait_ge(x_tr, nth(b - 2))
                    nc.vector.tensor_scalar(xn[:, r % 2, :], w.x_res[:, b, :], w.mean_var[:, b, 0:1], inv[:, 1, b, :],
                                            ALU.subtract, ALU.mult).then_inc(xn_done, 1)
                    dve.wait_ge(y_done, nth(b - 2))
                    nc.vector.scalar_tensor_tensor(out=u[0:T, r % 2, :], in0=ctx_u[:, b, :], scalar=inv[:, 0, b, :],
                                                   in1=g_init[:], op0=ALU.mult, op1=ALU.mult).then_inc(u_done, 1)

                def back(b, r):
                    dve.wait_ge(y_done, nth(b))
                    chain.link(nc.vector.tensor_tensor(w.x_res[:, b, :], w.bank(2 + r % 2, T, D), w.x_res[:, b, :],
                                                       ALU.add))
                    chain.link(statistics(nc, w, chain, stats[:, r, :], x_mv[:, r, :], w.x_res[:, b, :]))
                    alone(w, dve)
                    nc.vector.tensor_copy(w.mean_var[:, b, :], x_mv[:, r, :]).then_inc(x_done, 1)

                def body(i):
                    front(U * i, 0)
                    for r in range(1, U):
                        front(U * i + r, r)
                        back(U * i + r - 1, r - 1)
                    back(U * i + U - 1, U - 1)

                chain.loop(B // U, 3 * U, body)

            @block.scalar
            def _(act):
                for s in (x_t_done, m_done, squared):
                    act.sem_inc(s, CREDIT)
                for b in range(B):
                    r = b % U
                    act.wait_ge(ctx_in[r], 16 * (b // U + 1))
                    nc.scalar.activation(ctx_rows[:, r, :], ctx_rows[:, r, :], ACT.Square,
                                         accum_out=ms[:, 0, b:b + 1]).then_inc(squared, 1)
                act.wait_ge(ms_done, 1)
                nc.scalar.activation(root[:], ms[:], ACT.Sqrt).then_inc(root_done, 1)
                act.wait_ge(expo_done, 1)
                with act.Fori(0, B // U) as i:
                    for r in range(U):
                        b, k = U * i + r, r % 2
                        act.wait_ge(y_done, nth(b - 2))
                        nc.scalar.activation(m_scan[0:T, k, :], expo[:, bass.ds(b * T, T)], ACT.Exp).then_inc(m_done, 1)
                        act.wait_ge(x_tr, nth(b))
                        nc.scalar.activation(x_t[:, k, :, :], w.bank(k, P, KD * T).rearrange("p (k t) -> p k t", k=KD),
                                             ACT.Copy).then_inc(x_t_done, 1)

            @block.tensor
            def _(pe):
                for s in (x_tr, y_done):
                    pe.sem_inc(s, CREDIT)
                pe.wait_ge(idx_done, 1)
                for c in range(NQ):
                    last = nc.tensor.transpose(w.bank(0, CHUNK)[:, c * B:(c + 1) * B],
                                               idx[:, c * CHUNK:(c + 1) * CHUNK], w.ident[0:B, 0:B])
                last.then_inc(idx_tr, 1)
                pe.wait_ge(hit_done, 1)
                for g in range(NG):
                    for c in range(NQ):
                        last = nc.tensor.matmul(w.bank(g, T, GT), ones16[:], hit[:, c * B + g * GB:c * B + (g + 1) * GB, :],
                                                start=(c == 0), stop=(c == NQ - 1))
                last.then_inc(counted, 1)
                pe.wait_ge(expo_done, 1)
                with pe.Fori(0, B // U) as i:
                    def turn(b, r):
                        pe.wait_ge(xn_done, nth(b))
                        pe.wait_ge(x_t_done, nth(b - 2))
                        for kk in range(KD):
                            last = nc.tensor.transpose(w.bank(r % 2)[:, kk * T:(kk + 1) * T],
                                                       xn[:, r % 2, kk * P:(kk + 1) * P], w.ident[0:T, 0:T])
                        last.then_inc(x_tr, 1)

                    def product(b, r):
                        k = r % 2
                        y = w.bank(2 + k, T, D)
                        pe.wait_ge(x_t_done, nth(b))
                        pe.wait_ge(x_done, nth(b - 2))
                        for kk in range(KD):
                            nc.tensor.matmul(y, x_t[:, k, kk, :], w_in[:, kk, :], start=(kk == 0), stop=False)
                        pe.wait_ge(m_done, nth(b))
                        pe.wait_ge(u_done, nth(b))
                        nc.tensor.matmul(y, m_scan[0:T + 1, k, :], u[0:T + 1, k, :], start=False, stop=True).then_inc(y_done, 1)

                    turn(U * i, 0)
                    for r in range(1, U):
                        turn(U * i + r, r)
                        product(U * i + r - 1, r - 1)
                    product(U * i + U - 1, U - 1)

def stage2(w):
    nc, a = w.nc, w.a
    NM1, NM2 = KD * (P // ER), D // ER
    NM = NM1 + NM2
    PAIRS = B // 2
    with ExitStack() as ctx:
        sb = lambda n, s, d=F32: ctx.enter_context(nc.sbuf_tensor(n, s, d))
        sem = w.sem
        x_t = sb("s2_x_t", [P, KD, B * T])
        xn = sb("s2_xn", [T, 2, D])
        gate1 = sb("s2_gate1", [P, KD, D])
        gate1_b = sb("s2_gate1_b", [P, KD])
        gate2 = sb("s2_gate2", [P, KD, E])
        gate2_rep = sb("s2_gate2_rep", [P, KD, P])
        gate2_b = sb("s2_gate2_b", [E, 1])
        gate2_rep_b = sb("s2_gate2_rep_b", [P, 1])
        same_row = sb("s2_same_row", [P, ER])
        tb1 = sb("s2_tb1", [E + 1, F])
        tb2 = sb("s2_tb2", [E + 1, D])
        tmp = sb("s2_tmp", [T, B])
        root = sb("s2_root", [T, B])
        var = sb("s2_var", [T, B])
        hid = sb("s2_hid", [P, 2, GT])
        hid_sum = sb("s2_hid_sum", [P, KD, B])
        gate_er = sb("s2_gate_er", [P, B])
        gate_1 = sb("s2_gate_1", [E + 1, B])
        gate_1t = sb("s2_gate_1t", [E + 1, B, T])
        gate_sel = sb("s2_gate_sel", [P, B, ER])
        bias1 = sb("s2_bias1", [P, FC, B, 1])
        tw1 = sb("s2_tw1", [P, P // ER, D])
        tw2 = sb("s2_tw2", [P, D // ER, P])
        base1 = sb("s2_base1", [P, KD, P])
        base2 = sb("s2_base2", [P, D])
        m1 = sb("s2_m1", [P, KD, B, P])
        m2 = sb("s2_m2", [P, B, D])
        act_t = sb("s2_act_t", [P, B, T])

        loads = sem("s2_loads")
        tw1_in, tw2_in = sem("s2_tw1_in"), sem("s2_tw2_in")
        names = ("var_done", "root_done", "xn_done", "x_tr", "x_t_done", "hid_ps", "hid_done", "hid_sum_done",
                 "gate_ps", "gate_done", "gate_1t_done", "bias1_ps", "bias2_ps", "bias2_added", "merge_ps", "merged",
                 "h_ps", "act_done", "y_ps", "x_done", "chain", "achain", "sel_done", "bias1_done")
        S = {n: sem("s2_" + n) for n in names}

        pairs = [(gate1, "gate1_t"), (gate1_b, "gate1_b"), (gate2, "gate2_t"), (gate2_rep, "gate2_rep_t"),
                 (gate2_b, "gate2_b"), (gate2_rep_b, "gate2_rep_b"), (same_row, "same_row"), (tb1, "tb1"),
                 (tb2, "tb2")]
        N_LOADS = 16 * len(pairs)

        with nc.Block() as block:
            @block.sync
            def _(sp):
                for dst, name in pairs:
                    sp.dma_start(dst[:], a[name]).then_inc(loads, 16)

                def load(c, first):
                    if not first:
                        sp.wait_ge(S["merged"], nth(NM * (c - 1) + NM1 - 1))
                    sp.dma_start(tw1[:], a["tw1"][c]).then_inc(tw1_in, 16)
                    sp.dma_start(base1[:], a["w1_t"][c]).then_inc(tw1_in, 16)
                    if not first:
                        sp.wait_ge(S["merged"], nth(NM * (c - 1) + NM - 1))
                    sp.dma_start(tw2[:], a["tw2"][c]).then_inc(tw2_in, 16)
                    sp.dma_start(base2[:], a["w2_t"][c]).then_inc(tw2_in, 16)

                load(0, True)
                with sp.Fori(1, FC) as c:
                    load(c, False)

            @block.vector
            def _(dve):
                chain = Chain(dve, S["chain"])
                for n in ("xn_done", "hid_sum_done", "bias2_added", "merged", "x_done"):
                    dve.sem_inc(S[n], CREDIT)
                chain.link(nc.vector.memset(gate_1[:], 1.0))
                nc.vector.tensor_scalar(var[:], w.mean_var[:, :, 1], EPS, None, ALU.add).then_inc(S["var_done"], 1)
                dve.wait_ge(S["root_done"], 1)
                chain.link(inverse_root(nc, chain, w.rstd[:, :, 0], root[:], var[:], tmp[:]))

                def prepare(i):
                    for r in range(GB):
                        b = GB * i + r
                        dve.wait_ge(S["x_tr"], nth(b - 2))
                        normalised(nc, w, xn[:, r % 2, :], b).then_inc(S["xn_done"], 1)
                    for o in range(KD):
                        dve.wait_ge(S["hid_done"], nth(KD * i + o))
                        nc.vector.tensor_reduce(hid_sum[:, o, bass.ds(i * GB, GB)],
                                                hid[:, o, :].rearrange("p (b t) -> p b t", b=GB), AX.X,
                                                ALU.add).then_inc(S["hid_sum_done"], 1)

                chain.loop(NG, 0, prepare)
                dve.wait_ge(S["gate_done"], 2)
                chain.link(nc.vector.tensor_copy(gate_1t[:], gate_1[:].unsqueeze(2).broadcast_to([E + 1, B, T])))
                dve.sem_inc(S["gate_1t_done"], 1)
                nc.vector.tensor_tensor(gate_sel[:], gate_er[:].unsqueeze(2).broadcast_to([P, B, ER]),
                                        same_row[:].unsqueeze(1).broadcast_to([P, B, ER]), ALU.mult).then_inc(S["sel_done"], 1)
                dve.wait_ge(S["bias1_ps"], 1)
                nc.vector.tensor_copy(bias1[:].rearrange("p c b o -> p (c b o)"),
                                      w.bank(5, P, FC * B)).then_inc(S["bias1_done"], 1)
                for p in range(PAIRS):
                    dve.wait_ge(S["bias2_ps"], p + 1)
                    nc.vector.scalar_tensor_tensor(out=w.x_res[:, 2 * p:2 * p + 2, :],
                                                   in0=w.bank(6 + p % 2, T).rearrange("t (b d) -> t b d", b=2),
                                                   scalar=w.gates[0:T, 2:3], in1=w.x_res[:, 2 * p:2 * p + 2, :],
                                                   op0=ALU.mult, op1=ALU.add).then_inc(S["bias2_added"], 1)

                def chunk(c):
                    dve.wait_ge(tw1_in, 32 * (c + 1))
                    for n in range(NM):
                        if n == NM1:
                            dve.wait_ge(tw2_in, 32 * (c + 1))
                        dve.wait_ge(S["merge_ps"], nth(NM * c + n))
                        got = w.bank(n % 4).rearrange("p (b r) -> p b r", b=B)
                        if n < NM1:
                            q, kk = n // KD, n % KD
                            dst = m1[:, kk, :, q * ER:(q + 1) * ER]
                            base = base1[:, kk, q * ER:(q + 1) * ER]
                        else:
                            q = n - NM1
                            dst = m2[:, :, q * ER:(q + 1) * ER]
                            base = base2[:, q * ER:(q + 1) * ER]
                        nc.vector.tensor_tensor(dst, got, base.unsqueeze(1).broadcast_to([P, B, ER]),
                                                ALU.add).then_inc(S["merged"], 1)
                    for p in range(PAIRS):
                        dve.wait_ge(S["y_ps"], nth(PAIRS * c + p))
                        nc.vector.scalar_tensor_tensor(out=w.x_res[:, 2 * p:2 * p + 2, :],
                                                       in0=w.bank(6 + p % 2, T).rearrange("t (b d) -> t b d", b=2),
                                                       scalar=w.gates[0:T, 2:3], in1=w.x_res[:, 2 * p:2 * p + 2, :],
                                                       op0=ALU.mult, op1=ALU.add).then_inc(S["x_done"], 1)

                chain.loop(FC, 0, chunk)
                dve.wait_ge(S["x_done"], nth(PAIRS * FC - 1))
                row_statistics(nc, chain, w)

            @block.scalar
            def _(act):
                for n in ("x_t_done", "hid_done", "act_done"):
                    act.sem_inc(S[n], CREDIT)
                act.wait_ge(S["var_done"], 1)
                nc.scalar.activation(root[:], var[:], ACT.Sqrt).then_inc(S["root_done"], 1)
                act.wait_ge(loads, N_LOADS)
                with act.Fori(0, NG) as i:
                    for r in range(GB):
                        b = GB * i + r
                        act.wait_ge(S["x_tr"], nth(b))
                        nc.scalar.activation(x_t[:, :, bass.ds(b * T, T)],
                                             w.bank(r % 2, P, KD * T).rearrange("p (k t) -> p k t", k=KD),
                                             ACT.Copy).then_inc(S["x_t_done"], 1)
                    for o in range(KD):
                        act.wait_ge(S["hid_ps"], nth(KD * i + o))
                        act.wait_ge(S["hid_sum_done"], nth(KD * (i - 1) + o))
                        nc.scalar.activation(hid[:, o, :], w.bank(2 + o, P, GT), ACT.Relu,
                                             bias=gate1_b[:, o:o + 1]).then_inc(S["hid_done"], 1)
                act.wait_ge(S["gate_ps"], 1)
                nc.scalar.activation(gate_er[:], w.bank(4, P, B), ACT.Identity, bias=gate2_rep_b[:],
                                     scale=1.0 / T).then_inc(S["gate_done"], 1)
                nc.scalar.activation(gate_1[0:E, :], w.bank(4)[0:E, B:2 * B], ACT.Identity, bias=gate2_b[:],
                                     scale=1.0 / T).then_inc(S["gate_done"], 1)
                act.wait_ge(S["bias1_done"], 1)
                with act.Fori(0, FC) as c:
                    for g in range(NG):
                        act.wait_ge(S["h_ps"], nth(NG * c + g))
                        for r in range(GB):
                            b = GB * g + r
                            last = nc.scalar.activation(act_t[:, b, :], w.bank(4 + g % 2)[:, r * T:(r + 1) * T],
                                                        ACT.Gelu_apprx_tanh, bias=bias1[:, c, b, :])
                        last.then_inc(S["act_done"], 1)

            @block.tensor
            def _(pe):
                for n in ("x_tr", "hid_ps", "merge_ps", "h_ps", "y_ps"):
                    pe.sem_inc(S[n], CREDIT)
                pe.wait_ge(loads, N_LOADS)
                with pe.Fori(0, NG) as i:
                    for r in range(GB):
                        b = GB * i + r
                        pe.wait_ge(S["xn_done"], nth(b))
                        pe.wait_ge(S["x_t_done"], nth(b - 2))
                        for kk in range(KD):
                            last = nc.tensor.transpose(w.bank(r % 2)[:, kk * T:(kk + 1) * T],
                                                       xn[:, r % 2, kk * P:(kk + 1) * P], w.ident[0:T, 0:T])
                        last.then_inc(S["x_tr"], 1)
                    pe.wait_ge(S["x_t_done"], nth(GB * i + GB - 1))
                    for o in range(KD):
                        pe.wait_ge(S["hid_done"], nth(KD * (i - 1) + o))
                        for kk in range(KD):
                            last = nc.tensor.matmul(w.bank(2 + o, P, GT), gate1[:, kk, o * P:(o + 1) * P],
                                                    x_t[:, kk, bass.ds(i * GT, GT)], start=(kk == 0), stop=(kk == KD - 1))
                        last.then_inc(S["hid_ps"], 1)
                pe.wait_ge(S["hid_sum_done"], nth(KD * NG - 1))
                for kk in range(KD):
                    nc.tensor.matmul(w.bank(4, P, B), gate2_rep[:, kk, :], hid_sum[:, kk, :],
                                     start=(kk == 0), stop=(kk == KD - 1))
                for kk in range(KD):
                    last = nc.tensor.matmul(w.bank(4)[0:E, B:2 * B], gate2[:, kk, :], hid_sum[:, kk, :],
                                            start=(kk == 0), stop=(kk == KD - 1))
                last.then_inc(S["gate_ps"], 1)
                pe.wait_ge(S["gate_done"], 2)
                for c in range(FC):
                    last = nc.tensor.matmul(w.bank(5)[:, c * B:(c + 1) * B], tb1[:, c * P:(c + 1) * P], gate_1[:],
                                            start=True, stop=True)
                last.then_inc(S["bias1_ps"], 1)
                pe.wait_ge(S["gate_1t_done"], 1)
                for b in range(B):
                    p = b // 2
                    if b % 2 == 0 and p >= 2:
                        pe.wait_ge(S["bias2_added"], nth(p - 2))
                    last = nc.tensor.matmul(w.bank(6 + p % 2, T)[:, (b % 2) * D:(b % 2 + 1) * D], gate_1t[:, b, :], tb2[:],
                                            start=True, stop=True)
                    if b % 2:
                        last.then_inc(S["bias2_ps"], 1)
                pe.wait_ge(S["sel_done"], 1)
                pe.wait_ge(S["bias2_added"], nth(PAIRS - 1))
                sel = gate_sel[:].rearrange("p b r -> p (b r)")
                with pe.Fori(0, FC) as c:
                    for n in range(NM):
                        if n == 0:
                            pe.wait_ge(tw1_in, 32 * (c + 1))
                        if n == NM1:
                            pe.wait_ge(tw2_in, 32 * (c + 1))
                        pe.wait_ge(S["merged"], nth(NM * c + n - 4))
                        rows_ = tw1[:, n // KD, (n % KD) * P:(n % KD + 1) * P] if n < NM1 else tw2[:, n - NM1, :]
                        nc.tensor.matmul(w.bank(n % 4), rows_, sel, start=True, stop=True).then_inc(S["merge_ps"], 1)
                    pe.wait_ge(S["merged"], nth(NM * c + NM1 - 1))
                    for g in range(NG):
                        pe.wait_ge(S["act_done"], nth(NG * c + g - 2))
                        for r in range(GB):
                            b = GB * g + r
                            for kk in range(KD):
                                last = nc.tensor.matmul(w.bank(4 + g % 2)[:, r * T:(r + 1) * T], m1[:, kk, b, :],
                                                        x_t[:, kk, b * T:(b + 1) * T], start=(kk == 0), stop=(kk == KD - 1))
                        last.then_inc(S["h_ps"], 1)
                    pe.wait_ge(S["merged"], nth(NM * c + NM - 1))
                    for p in range(PAIRS):
                        pe.wait_ge(S["act_done"], nth(NG * c + p // 2))
                        pe.wait_ge(S["x_done"], nth(PAIRS * c + p - 2))
                        for r in range(2):
                            b = 2 * p + r
                            last = nc.tensor.matmul(w.bank(6 + p % 2, T)[:, r * D:(r + 1) * D], act_t[:, b, :], m2[:, b, :],
                                                    start=True, stop=True)
                        last.then_inc(S["y_ps"], 1)


def stage3(w):
    nc, a = w.nc, w.a
    TILE = HS * T
    K_OF = [CHUNK] * (NC - 1) + [T]
    HALVES = NC // 2
    NX = NT * HALVES
    NMX = H // 2
    MISC, OUT = 7, 6
    with ExitStack() as ctx:
        sb = lambda n, s, d=F32: ctx.enter_context(nc.sbuf_tensor(n, s, d))
        sem = w.sem
        wq = sb("s3_wq", [P, KD, NT, P])
        wk = sb("s3_wk", [P, KD, NT, P])
        wv = sb("s3_wv", [P, KD, D])
        w_proj = sb("s3_w_proj", [P, NT, D])
        shift_rows = sb("s3_shift_rows", [P, 1 + 2 * HS])
        xn = sb("s3_xn", [T, D])
        x_t = sb("s3_x_t", [P, KD, T])
        q_t = [sb(f"s3_q_t{k}", [P, NT, T]) for k in range(2)]
        q16 = sb("s3_q16", [P, NT, HS, T], BF16)
        q_m = sb("s3_q_m", [P, NT, HS, T])
        k_t = [sb(f"s3_k_t{k}", [P, NT, KPAD]) for k in range(2)]
        k16 = sb("s3_k16", [P, NT, NKEY], BF16)
        v_raw = [sb(f"s3_v_raw{k}", [CHUNK, NC - 1, D]) for k in range(2)]
        v = [sb(f"s3_v{k}", [CHUNK, NC, H, SLOT]) for k in range(2)]
        prob = [sb(f"s3_prob{k}", [CHUNK, NC, TILE]) for k in range(2)]
        neg_max = sb("s3_neg_max", [T, NT, HS, SLOT])
        o_t = [sb(f"s3_o_t{k}", [P, NT * T]) for k in range(2)]
        o_n = sb("s3_o_n", [P, NT * T])
        inv_den = sb("s3_inv_den", [T, H])
        inv_rep = sb("s3_inv_rep", [T, H, SLOT])
        stats, x_mv = sb("s3_stats", [T, 6]), sb("s3_x_mv", [T, 2])
        tmp, root, var = sb("s3_tmp", [T, B]), sb("s3_root", [T, B]), sb("s3_var", [T, B])

        loads = sem("s3_loads")
        keys_cleared, values_cleared = sem("s3_keys_cleared"), sem("s3_values_cleared")
        k_in = [sem(f"s3_k_in{k}") for k in range(2)]
        v_in = [sem(f"s3_v_in{k}") for k in range(2)]
        names = ("var_done", "root_done", "chain", "xn_done", "x_tr", "x_t_done", "q_ps", "q_done", "k_ps", "k_done",
                 "v_ps", "v_done", "q16_done", "k16_done", "v_put", "s16_ps", "max_done", "max_tr", "q_m_done",
                 "s_ps", "exp_done", "o_ps", "o_t_done", "den_ps", "inv_done", "inv_tr", "o_n_done", "y_ps", "x_done")
        S = {n: sem("s3_" + n) for n in names}
        weights = ((wq, "wq_t"), (wk, "wk_t"), (wv, "wv_t"), (w_proj, "w_proj_t"), (shift_rows, "shift_rows"))

        def turns(eng, turn, chain=None, per=0):
            turn(0, 0, 2, False, 0)

            def two(i):
                for n in range(2):
                    turn(2 * i + 1 + n, (1 + n) % 2, 2, True, i + 1)

            if chain is None:
                with eng.Fori(0, B // 2 - 2) as i:
                    two(i)
            else:
                chain.loop(B // 2 - 2, 2 * per, two)
            turn(B - 3, 1, 2, True, B // 2 - 1)
            turn(B - 2, 0, 1, True, B // 2 - 1)
            turn(B - 1, 1, 0, True, B // 2)

        with nc.Block() as block:
            @block.sync
            def _(sp):
                for dst, name in weights:
                    sp.dma_start(dst[:], a[name]).then_inc(loads, 16)
                sp.wait_ge(keys_cleared, 2)

                def load(b, k, first):
                    if not first:
                        sp.wait_ge(S["s_ps"], nth(NX * (b - 2) + NX - 1))
                    for s in range(HS):
                        sp.dma_start(k_t[k][s * SLOT:s * SLOT + DH, :, 0:S2], a["ctx_k_t"][b, s]).then_inc(k_in[k], 16)
                    if not first:
                        sp.wait_ge(S["v_put"], nth(b - 2))
                    sp.dma_start(v_raw[k][:], a["ctx"][b, :, D:2 * D].rearrange("(c p) d -> p c d", p=CHUNK))\
                        .then_inc(v_in[k], 16)

                for k in range(2):
                    load(k, k, True)
                with sp.Fori(1, B // 2) as i:
                    for k in range(2):
                        load(2 * i + k, k, False)

            @block.gpsimd
            def _(pool):
                pool.sem_inc(S["v_put"], CREDIT)
                for k in range(2):
                    nc.gpsimd.memset(v[k][:, :, :, 0:DH], 0.0)
                    nc.gpsimd.memset(v[k][:, :, :, DH + 1:SLOT], 0.0)
                    nc.gpsimd.memset(v[k][:, :, :, DH:DH + 1], 1.0)
                nc.gpsimd.memset(q16[:], 0.0).then_inc(values_cleared, 1)
                pool.wait_ge(values_cleared, 1)

                pool.wait_ge(loads, 16 * len(weights))

                def front(b, k, n):
                    pool.wait_ge(v_in[k], 16 * (n + 1))
                    pool.wait_ge(S["o_ps"], nth(NT * (b - 2) + NT - 1))
                    alone(w, pool)
                    nc.gpsimd.tensor_copy(v[k][:, 0:NC - 1, :, 0:DH],
                                          v_raw[k][:].rearrange("p c (h d) -> p c h d", h=H)).then_inc(S["v_put"], 1)

                front(0, 0, 0)
                front(1, 1, 0)
                with pool.Fori(1, B // 2) as i:
                    front(2 * i, 0, i)
                    front(2 * i + 1, 1, i)

            @block.scalar
            def _(act):
                for n in ("x_t_done", "q_done", "q16_done", "k16_done", "k_done", "v_done", "exp_done", "o_t_done"):
                    act.sem_inc(S[n], CREDIT)
                act.wait_ge(S["var_done"], 1)
                nc.scalar.activation(root[:], var[:], ACT.Sqrt).then_inc(S["root_done"], 1)
                act.wait_ge(loads, 16 * len(weights))
                act.wait_ge(keys_cleared, 2)
                act.wait_ge(values_cleared, 1)

                def evacuate_x(b):
                    act.wait_ge(S["x_tr"], nth(b))
                    nc.scalar.activation(x_t[:], w.bank(MISC, P, KD * T).rearrange("p (k t) -> p k t", k=KD),
                                         ACT.Copy).then_inc(S["x_t_done"], 1)

                def evacuate_q(b, k):
                    act.wait_ge(S["q_ps"], nth(b))
                    act.wait_ge(S["q_m_done"], nth(b - 2))
                    nc.scalar.activation(q_t[k][:], w.bank(0, P, NT * T).rearrange("p (n t) -> p n t", n=NT),
                                         ACT.Identity, scale=DH ** -0.5).then_inc(S["q_done"], 1)
                    act.wait_ge(S["s16_ps"], nth(NMX * (b - 1) + NMX - 1))
                    for s in range(HS):
                        rows_ = slice(s * SLOT, (s + 1) * SLOT)
                        last = nc.scalar.activation(q16[rows_, :, s, :],
                                                    w.banks[rows_, 0, 0:NT * T].rearrange("p (n t) -> p n t", n=NT),
                                                    ACT.Identity, scale=DH ** -0.5)
                    last.then_inc(S["q16_done"], 1)

                def evacuate_k(b, k):
                    act.wait_ge(S["k_ps"], nth(b))
                    got = w.bank(1, P, NT * T).rearrange("p (n t) -> p n t", n=NT)
                    nc.scalar.activation(k_t[k][:, :, S2:NKEY], got, ACT.Identity, bias=shift_rows[:, 0:1])
                    nc.scalar.activation(k16[:, :, S2:NKEY], got, ACT.Copy).then_inc(S["k_done"], 1)

                def evacuate_v(b, k):
                    act.wait_ge(S["v_ps"], nth(b))
                    nc.scalar.activation(v[k][0:T, NC - 1, :, 0:DH], w.bank(0, T, D).rearrange("p (h d) -> p h d", h=H),
                                         ACT.Copy).then_inc(S["v_done"], 1)

                def round_keys(b, k, n):
                    act.wait_ge(k_in[k], 16 * HS * (n + 1))
                    nc.scalar.activation(k16[:, :, 0:S2], k_t[k][:, :, 0:S2], ACT.Copy).then_inc(S["k16_done"], 1)

                def exp(b, t, h):
                    if h == 0:
                        act.wait_ge(S["o_ps"], nth(NT * b + t - 2))
                    act.wait_ge(S["s_ps"], nth(NX * b + HALVES * t + h))
                    nc.scalar.activation(prob[t % 2][:, 2 * h:2 * h + 2, :],
                                         w.banks[0:CHUNK, 2 + 2 * h:4 + 2 * h, 0:TILE], ACT.Exp).then_inc(S["exp_done"], 1)

                def turn(b, k, ahead, tail, used):
                    if ahead:
                        evacuate_q(b + 1, 1 - k)
                        evacuate_k(b + 1, 1 - k)
                        evacuate_v(b + 1, 1 - k)
                        round_keys(b + 1, 1 - k, used)
                    exp(b, 0, 0)
                    exp(b, 0, 1)
                    exp(b, 1, 0)
                    exp(b, 1, 1)
                    if ahead == 2:
                        evacuate_x(b + 2)
                    for t in range(2, NT):
                        exp(b, t, 0)
                        exp(b, t, 1)
                    act.wait_ge(S["o_ps"], nth(NT * b + NT - 1))
                    act.wait_ge(S["o_n_done"], nth(b - 2))
                    nc.scalar.activation(o_t[k][:], w.bank(OUT, P, NT * T), ACT.Copy).then_inc(S["o_t_done"], 1)

                evacuate_x(0)
                evacuate_q(0, 0)
                evacuate_k(0, 0)
                evacuate_v(0, 0)
                round_keys(0, 0, 0)
                evacuate_x(1)
                turns(act, turn)

            @block.vector
            def _(dve):
                chain = Chain(dve, S["chain"])
                for n in ("xn_done", "max_done", "q_m_done", "inv_done", "o_n_done", "x_done"):
                    dve.sem_inc(S[n], CREDIT)
                nc.vector.tensor_scalar(var[:], w.mean_var[:, :, 1], EPS, None, ALU.add).then_inc(S["var_done"], 1)
                nc.vector.memset(neg_max[:], 0.0)
                nc.vector.memset(q_m[:], 0.0)
                for k in range(2):
                    chain.link(nc.vector.memset(k_t[k][:], 0.0))
                dve.wait_ge(loads, 16 * len(weights))
                for k in range(2):
                    nc.vector.tensor_scalar(k_t[k][:, :, 0:NKEY], k_t[k][:, :, 0:NKEY], shift_rows[:, 0:1], None,
                                            ALU.add).then_inc(keys_cleared, 1)
                dve.wait_ge(S["root_done"], 1)
                chain.link(inverse_root(nc, chain, w.rstd[:, :, 0], root[:], var[:], tmp[:]))

                def norm(b):
                    dve.wait_ge(S["x_tr"], nth(b - 1))
                    normalised(nc, w, xn[:], b).then_inc(S["xn_done"], 1)

                def maximum(b, j):
                    if j == 0:
                        dve.wait_ge(S["max_tr"], nth(b - 1))
                    dve.wait_ge(S["s16_ps"], nth(NMX * b + j))
                    t, s = divmod(2 * j, HS)
                    nc.vector.tensor_reduce(neg_max[:, t, s:s + 2, DH:DH + 1], w.banks[0:T, 0:2, 0:NKEY], AX.X, ALU.max,
                                            negate=True).then_inc(S["max_done"], 1)

                def place_queries(b, k):
                    dve.wait_ge(S["max_tr"], nth(b))
                    for s in range(HS):
                        rows_ = slice(s * SLOT, (s + 1) * SLOT)
                        last = nc.vector.tensor_tensor(q_m[rows_, :, s, :],
                                                       w.banks[rows_, MISC, 0:NT * T].rearrange("p (n t) -> p n t", n=NT),
                                                       q_t[k][rows_, :, :], ALU.add)
                    last.then_inc(S["q_m_done"], 1)

                def invert(b):
                    dve.wait_ge(S["den_ps"], nth(b))
                    dve.wait_ge(S["inv_tr"], nth(b - 1))
                    chain.link(nc.vector.reciprocal(inv_den[:], w.bank(MISC, T, H)))
                    nc.vector.tensor_copy(inv_rep[:], inv_den[:].unsqueeze(2).broadcast_to([T, H, SLOT]))\
                        .then_inc(S["inv_done"], 1)

                def weigh(b, k):
                    dve.wait_ge(S["inv_tr"], nth(b))
                    nc.vector.tensor_tensor(o_n[:], o_t[k][:], w.bank(MISC, P, NT * T), ALU.mult).then_inc(S["o_n_done"], 1)

                def add(b):
                    dve.wait_ge(S["y_ps"], nth(b))
                    chain.link(nc.vector.scalar_tensor_tensor(out=w.x_res[:, b, :], in0=w.bank(MISC, T, D),
                                                              scalar=w.gates[0:T, 1:2], in1=w.x_res[:, b, :],
                                                              op0=ALU.mult, op1=ALU.add))
                    chain.link(statistics(nc, w, chain, stats[:], x_mv[:], w.x_res[:, b, :]))
                    alone(w, dve)
                    nc.vector.tensor_copy(w.mean_var[:, b, :], x_mv[:]).then_inc(S["x_done"], 1)

                def turn(b, k, ahead, tail, used):
                    place_queries(b, k)
                    if ahead == 2:
                        norm(b + 2)
                    for j in range(NMX):
                        if tail and j < 3:
                            (lambda: invert(b - 1), lambda: weigh(b - 1, 1 - k), lambda: add(b - 1))[j]()
                        if ahead:
                            maximum(b + 1, j)

                norm(0)
                norm(1)
                for j in range(NMX):
                    maximum(0, j)
                turns(dve, turn, chain, 4)
                invert(B - 1)
                weigh(B - 1, 1)
                add(B - 1)

            @block.tensor
            def _(pe):
                for n in ("x_tr", "q_ps", "k_ps", "v_ps", "s16_ps", "max_tr", "s_ps", "o_ps", "den_ps", "inv_tr", "y_ps"):
                    pe.sem_inc(S[n], CREDIT)
                pe.wait_ge(loads, 16 * len(weights))

                def turn_x(b):
                    pe.wait_ge(S["xn_done"], nth(b))
                    pe.wait_ge(S["x_done"], nth(b - 3))
                    pe.wait_ge(S["q_m_done"], nth(b - 2))
                    for kk in range(KD):
                        last = nc.tensor.transpose(w.bank(MISC)[:, kk * T:(kk + 1) * T], xn[:, kk * P:(kk + 1) * P],
                                                   w.ident[0:T, 0:T])
                    last.then_inc(S["x_tr"], 1)

                def project(weight, bank, signal):
                    for t in range(NT):
                        for kk in range(KD):
                            last = nc.tensor.matmul(w.bank(bank)[:, t * T:(t + 1) * T], weight[:, kk, t, :], x_t[:, kk, :],
                                                    start=(kk == 0), stop=(kk == KD - 1))
                    last.then_inc(S[signal], 1)

                def projections(b):
                    pe.wait_ge(S["x_t_done"], nth(b))
                    pe.wait_ge(S["max_done"], nth(NMX * (b - 1) + NMX - 1))
                    project(wq, 0, "q_ps")
                    project(wk, 1, "k_ps")
                    pe.wait_ge(S["q16_done"], nth(b))
                    for kk in range(KD):
                        last = nc.tensor.matmul(w.bank(0, T, D), x_t[:, kk, :], wv[:, kk, :],
                                                start=(kk == 0), stop=(kk == KD - 1))
                    last.then_inc(S["v_ps"], 1)

                def rough_scores(b, j):
                    if j == 0:
                        pe.wait_ge(S["v_done"], nth(b))
                        pe.wait_ge(S["k16_done"], nth(b))
                    pe.wait_ge(S["max_done"], nth(NMX * b + j - 1))
                    for n in range(2):
                        t, s = divmod(2 * j + n, HS)
                        last = nc.tensor.matmul(w.bank(n, T, NKEY), q16[:, t, s, :], k16[:, t, :], start=True, stop=True)
                    last.then_inc(S["s16_ps"], 1)

                def turn_maxima(b, ahead):
                    pe.wait_ge(S["max_done"], nth(NMX * b + NMX - 1))
                    if ahead:
                        pe.wait_ge(S["x_t_done"], nth(b + 1))
                    else:
                        pe.wait_ge(S["x_done"], nth(b - 2))
                    for t in range(NT):
                        last = nc.tensor.transpose(w.bank(MISC)[:, t * T:(t + 1) * T],
                                                   neg_max[:, t, :, :].rearrange("p s e -> p (s e)"), w.ident[0:T, 0:T])
                    last.then_inc(S["max_tr"], 1)

                def scores(b, k, t, h):
                    if t == 0 and h == 0:
                        pe.wait_ge(S["q_m_done"], nth(b))
                    pe.wait_ge(S["exp_done"], nth(NX * b + HALVES * t + h - 2))
                    for n in range(2):
                        c = 2 * h + n
                        last = nc.tensor.matmul(w.bank(2 + c, CHUNK, TILE), k_t[k][:, t, c * CHUNK:(c + 1) * CHUNK],
                                                q_m[:, t, :, :], start=True, stop=True)
                    last.then_inc(S["s_ps"], 1)

                def outputs(b, k, t):
                    if t == 0:
                        pe.wait_ge(S["o_t_done"], nth(b - 1))
                        pe.wait_ge(S["v_put"], nth(b))
                        pe.wait_ge(S["v_done"], nth(b))
                    pe.wait_ge(S["exp_done"], nth(NX * b + HALVES * t + 1))
                    for c in range(NC):
                        for s in range(HS):
                            last = nc.tensor.matmul(w.banks[s * SLOT:(s + 1) * SLOT, OUT, t * T:(t + 1) * T],
                                                    v[k][0:K_OF[c], c, t * HS + s, :],
                                                    prob[t % 2][0:K_OF[c], c, s * T:(s + 1) * T],
                                                    start=(c == 0), stop=(c == NC - 1))
                    last.then_inc(S["o_ps"], 1)

                def denominators(b, k, last_batch=False):
                    pe.wait_ge(S["o_t_done"], nth(b))
                    pe.wait_ge(S["x_done"], nth(b - 1))
                    if not last_batch:
                        pe.wait_ge(S["q_m_done"], nth(b + 1))
                    for t in range(NT):
                        last = nc.tensor.matmul(w.bank(MISC)[0:T, t * HS:(t + 1) * HS], o_t[k][:, t * T:(t + 1) * T],
                                                shift_rows[:, 1:1 + HS], start=True, stop=True)
                    last.then_inc(S["den_ps"], 1)

                def turn_inverses(b):
                    pe.wait_ge(S["inv_done"], nth(b))
                    for t in range(NT):
                        last = nc.tensor.transpose(w.bank(MISC)[:, t * T:(t + 1) * T],
                                                   inv_rep[:, t * HS:(t + 1) * HS, :].rearrange("p s e -> p (s e)"),
                                                   w.ident[0:T, 0:T])
                    last.then_inc(S["inv_tr"], 1)

                def project_out(b):
                    pe.wait_ge(S["o_n_done"], nth(b))
                    for t in range(NT):
                        last = nc.tensor.matmul(w.bank(MISC, T, D), o_n[:, t * T:(t + 1) * T], w_proj[:, t, :],
                                                start=(t == 0), stop=(t == NT - 1))
                    last.then_inc(S["y_ps"], 1)

                def turn(b, k, ahead, tail, used):
                    n = iter(range(NMX))

                    def rough():
                        if ahead:
                            rough_scores(b + 1, next(n))

                    turn_maxima(b, ahead)
                    if ahead:
                        projections(b + 1)
                    scores(b, k, 0, 0)
                    scores(b, k, 0, 1)
                    if tail:
                        denominators(b - 1, 1 - k)
                    rough()
                    scores(b, k, 1, 0)
                    if tail:
                        turn_inverses(b - 1)
                    rough()
                    scores(b, k, 1, 1)
                    if tail:
                        project_out(b - 1)
                    rough()
                    outputs(b, k, 0)
                    if ahead == 2:
                        turn_x(b + 2)
                    rough()
                    scores(b, k, 2, 0)
                    rough()
                    scores(b, k, 2, 1)
                    outputs(b, k, 1)
                    rough()
                    scores(b, k, 3, 0)
                    rough()
                    scores(b, k, 3, 1)
                    outputs(b, k, 2)
                    rough()
                    outputs(b, k, 3)

                turn_x(0)
                projections(0)
                turn_x(1)
                for j in range(NMX):
                    rough_scores(0, j)
                turns(pe, turn)
                denominators(B - 1, 1, last_batch=True)
                turn_inverses(B - 1)
                project_out(B - 1)

def stage4(w):
    nc, a = w.nc, w.a
    with ExitStack() as ctx:
        sb = lambda n, s, d=F32: ctx.enter_context(nc.sbuf_tensor(n, s, d))
        sem = w.sem
        xn = sb("s4_xn", [T, B, D])
        x_t = sb("s4_x_t", [P, KD, B * T])
        col_emb = sb("s4_col_emb", [C4, D])
        col_sq = sb("s4_col_sq", [C4, D])
        col_ss, col_root, col_inv = (sb("s4_col_" + n, [C4, 1]) for n in ("ss", "root", "inv"))
        col_tmp = sb("s4_col_tmp", [C4, 1])
        col_t = sb("s4_col_t", [P, KD, C4])
        cgate1 = sb("s4_cgate1", [P, KD, P])
        cgate1_b = sb("s4_cgate1_b", [P, 1])
        cgate2 = sb("s4_cgate2", [P, C4])
        cgate2_b = sb("s4_cgate2_b", [T, C4])
        w_cols = sb("s4_w_cols", [P, KD, F4])
        b_cols = sb("s4_b_cols", [P, J4])
        proj = sb("s4_proj", [P, J4, D])
        proj_b = sb("s4_proj_b", [T, D])
        ln_g = sb("s4_ln_g", [T, D])
        ln_b = sb("s4_ln_b", [T, D])
        col_of = sb("s4_col_of", [C4, F4])
        col_less = sb("s4_col_less", [P, C4])

        wts_t = sb("s4_wts_t", [C4, B * T])

        with ExitStack() as first:
            fb = lambda n, s, d=F32: first.enter_context(nc.sbuf_tensor(n, s, d))
            tmp, root, var = fb("s4_tmp", [T, B]), fb("s4_root", [T, B]), fb("s4_var", [T, B])
            xn_g = fb("s4_xn_g", [T, GB, D])
            x_g = fb("s4_x_g", [P, GB, KD, T])
            sq = fb("s4_sq", [T, GB, D])
            sumsq = fb("s4_sumsq", [T, B])
            hid = fb("s4_hid", [P, GT])
            logit, gate, eq, val = (fb("s4_" + n, [T, B, C4]) for n in ("logit", "gate", "eq", "val"))
            top, low, total = (fb("s4_" + n, [T, B]) for n in ("top", "low", "total"))
            loads = sem("s4_loads")
            late_loads = sem("s4_late_loads")
            names = ("var_done", "root_done", "chain", "xn_done", "x_tr", "x_g_done", "sq_done", "hid_ps", "hid_done",
                     "logit_ps", "logit_done", "ss_done", "ss_root", "sig_done", "diff_done", "exp_done", "wts_done", "wts_ps",
                     "col_ss_done", "col_ss_max", "col_root_done", "col_n_done", "col_ps", "col_t_done", "biased", "kept")
            S = {n: sem("s4_" + n) for n in names}
            early = ((col_emb[:], a["col_emb"]), (cgate1[:], a["cgate1"]), (cgate1_b[:], a["cgate1_b"]), (cgate2[:], a["cgate2"]),
                     (cgate2_b[:], a["cgate2_b"].partition_broadcast(T)), (col_less[:], a["col_less"]),
                     (proj_b[:], a["proj_b"].partition_broadcast(T)), (ln_g[:], a["ln_g"].partition_broadcast(T)),
                     (ln_b[:], a["ln_b"].partition_broadcast(T)))
            late = ((w_cols[:], a["w_cols"]), (b_cols[:], a["b_cols"]), (proj[:], a["proj"]), (col_of[:], a["col_of"]))

            with nc.Block() as block:
                @block.sync
                def _(sp):
                    for dst, src in early:
                        sp.dma_start(dst, src).then_inc(loads, 16)
                    for dst, src in late:
                        sp.dma_start(dst, src).then_inc(late_loads, 16)
                    sp.wait_ge(late_loads, 16 * len(late))

                @block.gpsimd
                def _(pool):
                    pool.wait_ge(loads, 16 * len(early))
                    pool.wait_ge(S["biased"], 1)
                    pool.sem_inc(S["kept"], CREDIT)
                    with pool.Fori(0, NG) as i:
                        for r in range(GB):
                            b = GB * i + r
                            pool.wait_ge(S["xn_done"], nth(b))
                            nc.gpsimd.tensor_tensor(w.x_res[:, b, :], w.x_res[:, b, :], ln_b[:], ALU.add)
                            nc.gpsimd.tensor_tensor(xn[:, b, :], xn_g[:, r, :], proj_b[:], ALU.add).then_inc(S["kept"], 1)

                @block.scalar
                def _(act):
                    for n in ("x_g_done", "sq_done", "hid_done"):
                        act.sem_inc(S[n], CREDIT)
                    act.wait_ge(loads, 16 * len(early))
                    nc.scalar.activation(col_sq[:], col_emb[:], ACT.Square, accum_out=col_ss[:]).then_inc(S["col_ss_done"], 1)
                    act.wait_ge(S["col_ss_max"], 1)
                    nc.scalar.activation(col_root[:], col_ss[:], ACT.Sqrt).then_inc(S["col_root_done"], 1)
                    act.wait_ge(S["var_done"], 1)
                    nc.scalar.activation(root[:], var[:], ACT.Sqrt).then_inc(S["root_done"], 1)
                    act.wait_ge(S["col_ps"], 1)
                    nc.scalar.activation(col_t[:], w.bank(4, P, KD * C4).rearrange("p (k c) -> p k c", k=KD),
                                         ACT.Copy).then_inc(S["col_t_done"], 1)
                    with act.Fori(0, NG) as i:
                        for r in range(GB):
                            b = GB * i + r
                            act.wait_ge(S["xn_done"], nth(b))
                            act.wait_ge(S["sq_done"], nth(b - GB))
                            nc.scalar.activation(sq[:, r, :], xn_g[:, r, :], ACT.Square,
                                                 accum_out=sumsq[:, bass.ds(b, 1)]).then_inc(S["sq_done"], 1)
                            act.wait_ge(S["x_tr"], nth(b))
                            got = w.bank(r % 2, P, KD * T).rearrange("p (k t) -> p k t", k=KD)
                            nc.scalar.activation(x_t[:, :, bass.ds(b * T, T)], got, ACT.Copy)
                            act.wait_ge(S["logit_ps"], nth(i - 1))
                            nc.scalar.activation(x_g[:, r, :, :], got, ACT.Copy).then_inc(S["x_g_done"], 1)
                        act.wait_ge(S["hid_ps"], nth(i))
                        nc.scalar.activation(hid[:], w.bank(2, P, GT), ACT.Gelu, bias=cgate1_b[:]).then_inc(S["hid_done"], 1)
                    act.wait_ge(S["ss_done"], 1)
                    nc.scalar.activation(root[:], sumsq[:], ACT.Sqrt).then_inc(S["ss_root"], 1)
                    nc.scalar.activation(gate[:], gate[:], ACT.Sigmoid).then_inc(S["sig_done"], 1)
                    act.wait_ge(S["diff_done"], 1)
                    nc.scalar.activation(logit[:], logit[:], ACT.Exp).then_inc(S["exp_done"], 1)
                    act.wait_ge(S["wts_ps"], 1)
                    for g in range(NG):
                        nc.scalar.activation(wts_t[:, g * GT:(g + 1) * GT], w.bank(g)[0:C4, 0:GT], ACT.Copy)

                @block.vector
                def _(dve):
                    chain = Chain(dve, S["chain"])
                    for n in ("xn_done", "logit_done"):
                        dve.sem_inc(S[n], CREDIT)
                    nc.vector.tensor_scalar(var[:], w.mean_var[:, :, 1], EPS, None, ALU.add).then_inc(S["var_done"], 1)
                    dve.wait_ge(loads, 16 * len(early))
                    chain.link(nc.vector.tensor_scalar(ln_g[:], ln_g[:], w.gates[0:T, 3:4], None, ALU.mult))
                    nc.vector.tensor_scalar(ln_b[:], ln_b[:], w.gates[0:T, 3:4], None, ALU.mult).then_inc(S["biased"], 1)
                    dve.wait_ge(S["col_ss_done"], 1)
                    nc.vector.tensor_scalar(col_ss[:], col_ss[:], 1e-24, None, ALU.max).then_inc(S["col_ss_max"], 1)
                    dve.wait_ge(S["col_root_done"], 1)
                    chain.link(inverse_root(nc, chain, col_inv[:], col_root[:], col_ss[:], col_tmp[:]))
                    nc.vector.tensor_scalar(col_emb[:], col_emb[:], col_inv[:], None, ALU.mult).then_inc(S["col_n_done"], 1)
                    dve.wait_ge(S["root_done"], 1)
                    chain.link(inverse_root(nc, chain, w.rstd[:, :, 0], root[:], var[:], tmp[:]))

                    def prepare(i):
                        for r in range(GB):
                            b = GB * i + r
                            dve.wait_ge(S["x_tr"], nth(b - GB))
                            dve.wait_ge(S["sq_done"], nth(b - GB))
                            dve.wait_ge(S["kept"], nth(b - GB))
                            normalised(nc, w, xn_g[:, r, :], b).then_inc(S["xn_done"], 1)
                        dve.wait_ge(S["logit_ps"], nth(i))
                        got = w.bank(3, T, GB * 2 * C4).rearrange("p (b c) -> p b c", b=GB)
                        nc.vector.tensor_tensor(gate[:, bass.ds(i * GB, GB), :], got[:, :, 0:C4],
                                                cgate2_b[:].unsqueeze(1).broadcast_to([T, GB, C4]), ALU.add)
                        nc.vector.tensor_copy(logit[:, bass.ds(i * GB, GB), :], got[:, :, C4:2 * C4])\
                            .then_inc(S["logit_done"], 1)

                    chain.loop(NG, 0, prepare)
                    dve.wait_ge(S["logit_done"], nth(NG - 1))
                    dve.wait_ge(S["sq_done"], nth(B - 1))
                    nc.vector.tensor_scalar(sumsq[:], sumsq[:], 1e-24, None, ALU.max).then_inc(S["ss_done"], 1)
                    dve.wait_ge(S["ss_root"], 1)
                    chain.link(inverse_root(nc, chain, top[:], root[:], sumsq[:], tmp[:]))

                    def each(v):
                        return v[:].unsqueeze(2).broadcast_to([T, B, C4])

                    chain.link(nc.vector.tensor_tensor(logit[:], logit[:], each(top), ALU.mult))
                    dve.wait_ge(S["sig_done"], 1)
                    chain.link(nc.vector.tensor_tensor(logit[:], logit[:], gate[:], ALU.add))
                    chain.link(nc.vector.tensor_reduce(top[:], logit[:], AX.X, ALU.max))
                    chain.link(nc.vector.tensor_tensor(eq[:], logit[:], each(top), ALU.is_equal))
                    nc.vector.tensor_tensor(logit[:], logit[:], each(top), ALU.subtract).then_inc(S["diff_done"], 1)
                    chain.link(nc.vector.tensor_tensor(val[:], eq[:], col_less[0:T, :].unsqueeze(1).broadcast_to([T, B, C4]),
                                                       ALU.mult))
                    chain.link(nc.vector.tensor_reduce(low[:], val[:], AX.X, ALU.min))
                    chain.link(nc.vector.tensor_tensor(eq[:], val[:], each(low), ALU.is_equal))
                    dve.wait_ge(S["exp_done"], 1)
                    chain.link(nc.vector.tensor_reduce(total[:], logit[:], AX.X, ALU.add))
                    chain.link(nc.vector.reciprocal(total[:], total[:]))
                    chain.link(nc.vector.tensor_tensor(val[:], logit[:], eq[:], ALU.mult))
                    nc.vector.tensor_tensor(val[:], val[:], each(total), ALU.mult).then_inc(S["wts_done"], 1)

                @block.tensor
                def _(pe):
                    for n in ("x_tr", "hid_ps", "logit_ps"):
                        pe.sem_inc(S[n], CREDIT)
                    pe.wait_ge(S["col_n_done"], 1)
                    for kk in range(KD):
                        last = nc.tensor.transpose(w.bank(4)[:, kk * C4:(kk + 1) * C4], col_emb[:, kk * P:(kk + 1) * P],
                                                   w.ident[0:C4, 0:C4])
                    last.then_inc(S["col_ps"], 1)
                    pe.wait_ge(S["col_t_done"], 1)
                    with pe.Fori(0, NG) as i:
                        for r in range(GB):
                            b = GB * i + r
                            pe.wait_ge(S["xn_done"], nth(b))
                            pe.wait_ge(S["x_g_done"], nth(b - 2))
                            for kk in range(KD):
                                last = nc.tensor.transpose(w.bank(r % 2)[:, kk * T:(kk + 1) * T],
                                                           xn_g[:, r, kk * P:(kk + 1) * P], w.ident[0:T, 0:T])
                            last.then_inc(S["x_tr"], 1)
                        pe.wait_ge(S["x_g_done"], nth(GB * i + GB - 1))
                        pe.wait_ge(S["hid_done"], nth(i - 1))
                        for kk in range(KD):
                            last = nc.tensor.matmul(w.bank(2, P, GT), cgate1[:, kk, :], x_g[:, :, kk, :],
                                                    start=(kk == 0), stop=(kk == KD - 1))
                        last.then_inc(S["hid_ps"], 1)
                        pe.wait_ge(S["logit_done"], nth(i - 1))
                        pe.wait_ge(S["hid_done"], nth(i))
                        for r in range(GB):
                            at = r * 2 * C4
                            nc.tensor.matmul(w.bank(3, T)[:, at:at + C4], hid[:, r * T:(r + 1) * T], cgate2[:],
                                             start=True, stop=True)
                            for kk in range(KD):
                                last = nc.tensor.matmul(w.bank(3, T)[:, at + C4:at + 2 * C4], x_g[:, r, kk, :],
                                                        col_t[:, kk, :], start=(kk == 0), stop=(kk == KD - 1))
                        last.then_inc(S["logit_ps"], 1)
                    pe.wait_ge(S["wts_done"], 1)
                    for b in range(B):
                        last = nc.tensor.transpose(w.bank(b // GB)[0:C4, (b % GB) * T:(b % GB + 1) * T], val[:, b, :],
                                                   w.ident[0:T, 0:T])
                    last.then_inc(S["wts_ps"], 1)

        hid_c = [sb(f"s4_hid_c{n}", [P, GT]) for n in range(2)]
        weighted = [sb(f"s4_weighted{n}", [P, J4, GT]) for n in range(2)]
        res = [sb(f"s4_res{n}", [T, GB, D]) for n in range(2)]
        stats = sb("s4_stats", [T, GB, 6])
        y_mv = [sb(f"s4_y_mv{n}", [T, GB, 2]) for n in range(2)]
        y_var, y_root, y_inv, y_tmp = (sb("s4_y_" + n, [T, GB]) for n in ("var", "root", "inv", "tmp"))
        names = ("col_ps", "gelu_done", "weigh_done", "y_ps", "y_done", "y_var_done", "y_root_done", "res_done", "chain2")
        S = {n: sem("s4b_" + n) for n in names}
        stored = [sem(f"s4_stored{k}") for k in range(2)]

        def turns(turn, eng=None, chain=None, per=0):
            turn(0, 0, False, 0)

            def two(i):
                turn(2 * i + 1, 1, True, i)
                turn(2 * i + 2, 0, True, i)

            if chain is None:
                with eng.Fori(0, NG // 2 - 1) as i:
                    two(i)
            else:
                chain.loop(NG // 2 - 1, 2 * per, two)
            turn(NG - 1, 1, True, NG // 2 - 1)

        with nc.Block() as block:
            @block.sync
            def _(sp):
                with sp.Fori(0, NG // 2) as i:
                    for k in range(2):
                        g = 2 * i + k
                        sp.wait_ge(S["res_done"], nth(g))
                        sp.dma_start(w.out[bass.ds(g * GB, GB)].rearrange("b t d -> t b d"), res[k][:]).then_inc(stored[k], 16)
                for k in range(2):
                    sp.wait_ge(stored[k], 16 * (NG // 2))

            @block.scalar
            def _(act):
                for n in ("gelu_done", "y_root_done"):
                    act.sem_inc(S[n], CREDIT)

                def norm_root(g):
                    act.wait_ge(S["y_var_done"], nth(g))
                    nc.scalar.activation(y_root[:], y_var[:], ACT.Sqrt).then_inc(S["y_root_done"], 1)

                def turn(g, k, tail, n):
                    for j in range(J4):
                        act.wait_ge(S["col_ps"], nth(J4 * g + j))
                        act.wait_ge(S["weigh_done"], nth(J4 * g + j - 2))
                        nc.scalar.activation(hid_c[j % 2][:], w.bank(j % 2, P, GT), ACT.Gelu,
                                             bias=b_cols[:, j:j + 1]).then_inc(S["gelu_done"], 1)
                    if tail:
                        norm_root(g - 1)

                turns(turn, act)
                norm_root(NG - 1)

            @block.vector
            def _(dve):
                chain = Chain(dve, S["chain2"])
                for n in ("weigh_done", "y_done", "y_var_done", "res_done"):
                    dve.sem_inc(S[n], CREDIT)

                def weigh(g, k, j):
                    if j == 0:
                        dve.wait_ge(S["y_ps"], nth(GB * (g - 2) + GB - 1))
                    dve.wait_ge(S["gelu_done"], nth(J4 * g + j))
                    nc.vector.tensor_tensor(weighted[k][:, j, :], hid_c[j % 2][:], w.bank(2 + j % 2, P, GT),
                                            ALU.mult).then_inc(S["weigh_done"], 1)

                def residual(g, k, r):
                    b = GB * g + r
                    dve.wait_ge(S["y_ps"], nth(b))
                    chain.link(nc.vector.tensor_tensor(xn[:, b, :], w.bank(4 + r, T, D), xn[:, b, :], ALU.add))
                    statistics(nc, w, chain, stats[:, r, :], y_mv[k][:, r, :], xn[:, b, :]).then_inc(S["y_done"], 1)

                def variance(g, k):
                    dve.wait_ge(S["y_done"], nth(GB * g + GB - 1))
                    nc.vector.tensor_scalar(y_var[:], y_mv[k][:, :, 1], EPS, None, ALU.add).then_inc(S["y_var_done"], 1)

                def finish(g, k, n):
                    dve.wait_ge(S["y_root_done"], nth(g))
                    chain.link(inverse_root(nc, chain, y_inv[:], y_root[:], y_var[:], y_tmp[:]))
                    dve.wait_ge(stored[k], 16 * n)
                    for r in range(GB):
                        last = nc.vector.tensor_scalar(res[k][:, r, :], xn[:, GB * g + r, :], y_mv[k][:, r, 0:1],
                                                       y_inv[:, r:r + 1], ALU.subtract, ALU.mult)
                    chain.link(last)
                    chain.link(nc.vector.tensor_tensor(res[k][:], res[k][:], ln_g[:].unsqueeze(1).broadcast_to([T, GB, D]),
                                                       ALU.mult))
                    nc.vector.tensor_tensor(res[k][:], res[k][:], w.x_res[:, bass.ds(GB * g, GB), :], ALU.add)\
                        .then_inc(S["res_done"], 1)

                def turn(g, k, tail, n):
                    for j in range(J4):
                        weigh(g, k, j)
                        if tail and j % 2:
                            residual(g - 1, 1 - k, j // 2)
                    if tail:
                        variance(g - 1, 1 - k)
                        finish(g - 1, 1 - k, n)

                turns(turn, None, chain, 2 * GB + 7)
                for r in range(GB):
                    residual(NG - 1, 1, r)
                variance(NG - 1, 1)
                finish(NG - 1, 1, NG // 2 - 1)

            @block.tensor
            def _(pe):
                for n in ("col_ps", "y_ps"):
                    pe.sem_inc(S[n], CREDIT)

                def columns(g, j):
                    pe.wait_ge(S["weigh_done"], nth(J4 * g + j - 2))
                    alone(w, pe)
                    nc.tensor.matmul(w.bank(2 + j % 2, P, GT), col_of[:, j * P:(j + 1) * P], wts_t[:, bass.ds(g * GT, GT)],
                                     start=True, stop=True)
                    for kk in range(KD):
                        last = nc.tensor.matmul(w.bank(j % 2, P, GT), w_cols[:, kk, j * P:(j + 1) * P],
                                                x_t[:, kk, bass.ds(g * GT, GT)], start=(kk == 0), stop=(kk == KD - 1))
                    last.then_inc(S["col_ps"], 1)

                def output(g, k, r):
                    if r == 0:
                        pe.wait_ge(S["weigh_done"], nth(J4 * g + J4 - 1))
                    pe.wait_ge(S["y_done"], nth(GB * (g - 1) + r))
                    for j in range(J4):
                        last = nc.tensor.matmul(w.bank(4 + r, T, D), weighted[k][:, j, r * T:(r + 1) * T], proj[:, j, :],
                                                start=(j == 0), stop=(j == J4 - 1))
                    last.then_inc(S["y_ps"], 1)

                def turn(g, k, tail, n):
                    for j in range(J4):
                        columns(g, j)
                        if tail and j % 2:
                            output(g - 1, 1 - k, j // 2)

                turns(turn, pe)
                for r in range(GB):
                    output(NG - 1, 1, r)



def lay_out(x, ctx_2048, mask_BxS2_if0, g_xattn, g_ffn, L0_xattn_W_in, L0_xattn_b_in, L0_xattn_g_res,
            L0_xattn_g_init, L0_ffn_gate_w1, L0_ffn_gate_b1, L0_ffn_gate_w2, L0_ffn_gate_b2, L0_ffn_W1,
            L0_ffn_b1, L0_ffn_W2, L0_ffn_b2, L0_ffn_TW1, L0_ffn_Tb1, L0_ffn_TW2, L0_ffn_Tb2, L1_xattn_w_qkv,
            L1_xattn_w_proj, L1_xattn_b_proj, L1_ffn_col_emb, L1_ffn_gate_w1, L1_ffn_gate_b1, L1_ffn_gate_w2,
            L1_ffn_gate_b2, L1_ffn_W_cols, L1_ffn_b_cols, L1_ffn_proj_w, L1_ffn_proj_b, L1_ffn_ln_g,
            L1_ffn_ln_b):
    f32 = np.float32

    def rows(m):
        m = np.asarray(m)
        return m.reshape(-1, P, m.shape[-1]).transpose(1, 0, 2)

    def column(v):
        return np.asarray(v).reshape(-1, P).T

    out = {"x": x, "ctx": ctx_2048, "mask": mask_BxS2_if0, "g_xattn": g_xattn, "g_ffn": g_ffn}
    out["ident"] = np.eye(P, dtype=f32)
    out["iota"] = np.concatenate([np.tile(np.arange(T), (P, 1)), np.arange(P)[:, None]], 1).astype(f32)
    out["w_in_t"] = rows(np.asarray(L0_xattn_W_in).T)
    out["g_res_c"] = column(L0_xattn_g_res)
    out["g_init_row"] = np.asarray(L0_xattn_g_init)[:D]
    out["b_in_row"] = np.asarray(L0_xattn_b_in)[None]
    out["gate1_t"] = rows(np.asarray(L0_ffn_gate_w1).T)
    out["gate1_b"] = column(L0_ffn_gate_b1)
    gate2_t = np.asarray(L0_ffn_gate_w2).T
    out["gate2_t"] = rows(gate2_t)
    out["gate2_rep_t"] = rows(np.repeat(gate2_t, ER, 1))
    out["gate2_b"] = np.asarray(L0_ffn_gate_b2)[:, None]
    out["gate2_rep_b"] = np.repeat(np.asarray(L0_ffn_gate_b2), ER)[:, None]
    out["same_row"] = np.tile(np.eye(ER, dtype=f32), (E, 1))
    tw1 = np.asarray(L0_ffn_TW1).reshape(E, FC, P // ER, ER, D)
    out["tw1"] = tw1.transpose(1, 0, 3, 2, 4).reshape(FC, P, P // ER, D)
    tw2 = np.asarray(L0_ffn_TW2).reshape(E, D // ER, ER, FC, P)
    out["tw2"] = tw2.transpose(3, 0, 2, 1, 4).reshape(FC, P, D // ER, P)
    out["w1_t"] = np.asarray(L0_ffn_W1).T.reshape(KD, P, FC, P).transpose(2, 1, 0, 3)
    out["w2_t"] = np.asarray(L0_ffn_W2).T.reshape(FC, P, D)
    out["tb1"] = np.concatenate([np.asarray(L0_ffn_Tb1), np.asarray(L0_ffn_b1)[None]])
    out["tb2"] = np.concatenate([np.asarray(L0_ffn_Tb2), np.asarray(L0_ffn_b2)[None]])
    w_qkv = np.asarray(L1_xattn_w_qkv)
    for name, part in (("wq_t", w_qkv[:D]), ("wk_t", w_qkv[D:2 * D])):
        slots = np.zeros((D, NT, HS, SLOT), f32)
        slots[:, :, :, :DH] = part.T.reshape(D, NT, HS, DH)
        out[name] = slots.reshape(KD, P, NT, P).transpose(1, 0, 2, 3)
    out["wv_t"] = rows(w_qkv[2 * D:].T)
    out["ctx_k_t"] = np.asarray(ctx_2048)[:, :, :D].reshape(B, S2, NT, HS, DH).transpose(0, 3, 4, 2, 1)
    slots = np.zeros((NT, HS, SLOT, D), f32)
    slots[:, :, :DH] = np.asarray(L1_xattn_w_proj).T.reshape(NT, HS, DH, D)
    slots[0, 0, DH] = np.asarray(L1_xattn_b_proj)
    out["w_proj_t"] = slots.reshape(NT, P, D).transpose(1, 0, 2)
    aug = np.zeros((P, 1 + 2 * HS), f32)
    aug[DH::SLOT, 0] = 1
    for s in range(HS):
        aug[s * SLOT + DH, 1 + s] = 1
        aug[s * SLOT:(s + 1) * SLOT, 1 + HS + s] = 1
    out["shift_rows"] = aug
    out["col_emb"] = L1_ffn_col_emb
    out["cgate1"] = rows(L1_ffn_gate_w1)
    out["cgate1_b"] = column(L1_ffn_gate_b1)
    out["cgate2"] = L1_ffn_gate_w2
    out["cgate2_b"] = L1_ffn_gate_b2
    out["w_cols"] = rows(np.asarray(L1_ffn_W_cols).transpose(1, 0, 2).reshape(D, F4))
    out["b_cols"] = column(np.asarray(L1_ffn_b_cols).reshape(-1))
    out["proj"] = rows(L1_ffn_proj_w)
    out["proj_b"] = L1_ffn_proj_b
    out["ln_g"] = L1_ffn_ln_g
    out["ln_b"] = L1_ffn_ln_b
    out["col_of"] = np.repeat(np.eye(C4, dtype=f32), N4, 1)
    out["col_less"] = np.tile(np.arange(C4) - float(C4), (P, 1)).astype(f32)
    return {k: np.ascontiguousarray(v) for k, v in out.items()}


def kernel(**inputs):
    import concourse.bacc as bacc
    from concourse.bass_utils import run_bass_kernel_spmd

    nc = bacc.Bacc("TRN2", target_bir_lowering=False, num_devices=1)
    arrays = {f"in_{k}": v for k, v in lay_out(**inputs).items()}
    a = {k[3:]: nc.dram_tensor(k, v.shape, mybir.dt.from_np(v.dtype), kind="ExternalInput").ap()
         for k, v in arrays.items()}
    out = nc.dram_tensor("out_x", (B, T, D), F32, kind="ExternalOutput").ap()
    build(nc, a, out)
    return run_bass_kernel_spmd(nc, [arrays], core_ids=[0]).results[0]["out_x"]
```

```python
from contextlib import ExitStack

import concourse.bass as bass
from concourse import mybir
import numpy as np

ALU = mybir.AluOpType
ACT = mybir.ActivationFunctionType
AX = mybir.AxisListType
F32 = mybir.dt.float32
BF16 = mybir.dt.bfloat16
I32 = mybir.dt.int32

B, T, D = 32, 112, 256
S2, DC = 375, 512
P = 128
KD = D // P
GB = 4
NG = B // GB
GT = GB * T
CHUNK = 125
NC = S2 // CHUNK + 1
KPAD = NC * CHUNK
NKEY = S2 + T
EPS = 1e-5
F, E = 1024, 8
ER = P // E
FC = F // P
H, DH, SLOT = 16, 16, 32
HS = P // SLOT
NT = H // HS
C4, N4 = 16, 64
F4 = C4 * N4
J4 = F4 // P
DEPOOL_EPS = 0.001
CREDIT = 4


def nth(n):
    return n + (1 + CREDIT)


class Chain:

    def __init__(self, eng, sem):
        self.eng, self.sem, self.base, self.k = eng, sem, 0, 0

    def link(self, ins):
        self.k += 1
        ins.then_inc(self.sem, 1)
        self.eng.wait_ge(self.sem, self.base + self.k)

    def loop(self, count, per, body):
        start = self.base + self.k
        with self.eng.Fori(0, count) as i:
            self.base, self.k = start + i * per, 0
            body(i)
            assert self.k == per, (self.k, per)
        self.base, self.k = start + count * per, 0


def alone(w, eng):
    eng.sem_inc(w.carried, 1)


def statistics(nc, w, chain, stats, mean_var, x):
    alone(w, chain.eng)
    chain.link(nc.vector.bn_stats(stats, x))
    alone(w, chain.eng)
    return nc.vector.bn_aggr(mean_var, stats)


def inverse_root(nc, chain, out, root, v, tmp):
    chain.link(nc.vector.reciprocal(out, root))
    chain.link(nc.vector.tensor_tensor(tmp, out, out, ALU.mult))
    chain.link(nc.vector.tensor_tensor(tmp, tmp, v, ALU.mult))
    chain.link(nc.vector.tensor_scalar(tmp, tmp, -0.5, 1.5, ALU.mult, ALU.add))
    return nc.vector.tensor_tensor(out, out, tmp, ALU.mult)


def normalised(nc, w, out, b):
    return nc.vector.tensor_scalar(out, w.x_res[:, b, :], w.mean_var[:, b, 0:1], w.rstd[:, b, :],
                                   ALU.subtract, ALU.mult)


def build(nc, a, out):
    ctx = ExitStack()
    with ctx:
        world = World(nc, a, out, ctx)
        setup(world)
        stage1(world)
        stage2(world)
        stage3(world)
        stage4(world)


class World:

    def __init__(self, nc, a, out, ctx):
        self.nc, self.a, self.out, self.ctx = nc, a, out, ctx
        sb = lambda n, s, d=F32: ctx.enter_context(nc.sbuf_tensor(n, s, d))
        self.x_res = sb("x_res", [T, B, D])
        self.mean_var = sb("mean_var", [T, B, 2])
        self.rstd = sb("rstd", [T, B, 1])
        self.ident = sb("ident", [P, P])
        self.gates = sb("gates", [P, 4])
        self.x_in = [self.sem(f"x_in{g}") for g in range(NG)]
        self.banks = ctx.enter_context(nc.psum_tensor("banks", [P, 8, 512], F32))
        self.attention = {"wq_t": sb("s3_wq", [P, KD, NT, P]), "wk_t": sb("s3_wk", [P, KD, NT, P]),
                          "wv_t": sb("s3_wv", [P, KD, D]), "w_proj_t": sb("s3_w_proj", [P, NT, D]),
                          "shift_rows": sb("s3_shift_rows", [P, 1 + 2 * HS])}
        self.attention_in = self.sem("attention_in")
        self.carried = self.sem("carried")

    def sem(self, name):
        return self.ctx.enter_context(self.nc.semaphore(name))

    def bank(self, n, parts=P, cols=512):
        return self.banks[0:parts, n, 0:cols]


def load_x(w, sp):
    for g in range(NG):
        sp.dma_start(w.x_res[:, g * GB:(g + 1) * GB, :],
                     w.a["x"][g * GB:(g + 1) * GB].rearrange("b t d -> t b d")).then_inc(w.x_in[g], 16)


def load_attention(w, sp):
    for name, dst in w.attention.items():
        sp.dma_start(dst[:], w.a[name]).then_inc(w.attention_in, 16)


def setup(w):
    nc, a = w.nc, w.a
    consts_in, graw_in = w.sem("consts_in"), w.sem("graw_in")
    with nc.sbuf_tensor("gates_raw", [P, 4], F32) as gates_raw, nc.Block() as block:
        @block.sync
        def _(sp):
            for n, g in enumerate((a["g_xattn"], a["g_ffn"])):
                sp.dma_start(gates_raw[:, 2 * n:2 * n + 2], g.partition_broadcast(P)).then_inc(graw_in, 16)
            sp.dma_start(w.ident[:], a["ident"]).then_inc(consts_in, 16)
            sp.wait_ge(consts_in, 16)

        @block.scalar
        def _(act):
            act.wait_ge(graw_in, 32)
            nc.scalar.activation(w.gates[:], gates_raw[:], ACT.Tanh)


def stage1(w):
    nc, a = w.nc, w.a
    dt = float(-np.log(-np.expm1(-DEPOOL_EPS)))
    bcoef = float(np.exp(-DEPOOL_EPS))
    NQ = S2 // CHUNK
    U = 4
    with ExitStack() as ctx:
        sb = lambda n, s, d=F32: ctx.enter_context(nc.sbuf_tensor(n, s, d))
        sem = w.sem
        w_in = sb("s1_w_in", [P, KD, D])
        g_res = sb("s1_g_res", [P, KD])
        g_init = sb("s1_g_init", [T, D])
        mask_i = sb("s1_mask_i", [B, S2], I32)
        mask_f = sb("s1_mask_f", [B, S2])
        zero = sb("s1_zero", [B, S2])
        cum = sb("s1_cum", [B, S2])
        idx = sb("s1_idx", [B, S2])
        wrap = sb("s1_wrap", [B, S2])
        idx_t = sb("s1_idx_t", [CHUNK, NQ * B])
        iota = sb("s1_iota", [P, T + 1])
        ones16 = sb("s1_ones16", [CHUNK, T], BF16)
        hit = sb("s1_hit", [CHUNK, NQ * B, T], BF16)
        mark = sb("s1_mark", [T, B * T])
        keep = sb("s1_keep", [T, B, T])
        plug = sb("s1_plug", [T, B * T])
        pos, expo = mark, plug
        ctx_u = sb("s1_ctx_u", [T, B, D])
        ctx_v = sb("s1_ctx_v", [T, 2, GB, D])
        squares = sb("s1_squares", [T, 2, D])
        halves = sb("s1_halves", [T, 2, B])
        ms = sb("s1_ms", [T, 2, B])
        root = sb("s1_root", [T, 2, B])
        inv = sb("s1_inv", [T, 2, B, 1])
        tmp = sb("s1_tmp", [T, 2, B])
        u = sb("s1_u", [P, U, D])
        m_scan = sb("s1_m_scan", [P, U, T])
        xn = sb("s1_xn", [T, U, D])
        x_t = sb("s1_x_t", [P, U, KD, T])
        stats = sb("s1_stats", [T, B, 6])
        x_mv = sb("s1_x_mv", [T, U, 2])
        table = sb("s1_table", [P, 1])

        loads, mask_in, bias_in = sem("s1_loads"), sem("s1_mask_in"), sem("s1_bias_in")
        ctx_v_in = [sem(f"s1_ctx_v_in{k}") for k in range(2)]
        cleared, idx_done, idx_tr, hit_done, counted = (sem("s1_" + n) for n in (
            "cleared", "idx_done", "idx_tr", "hit_done", "counted"))
        prep, expo_done = sem("s1_prep"), sem("s1_expo_done")
        xn_done, x_tr, x_t_done, m_done = (sem("s1_" + n) for n in ("xn_done", "x_tr", "x_t_done", "m_done"))
        squared, ms_done, root_done, u_done, y_done, x_done, chain_s = (sem("s1_" + n) for n in (
            "squared", "ms_done", "root_done", "u_done", "y_done", "x_done", "chain"))
        ctx_u_in = [sem(f"s1_ctx_u_in{g}") for g in range(NG)]

        with nc.Block() as block:
            @block.sync
            def _(sp):
                sp.dma_start(mask_i[:], a["mask"]).then_inc(mask_in, 16)
                for dst, src in ((iota[:], a["iota"]), (w_in[:], a["w_in_t"]), (g_res[:], a["g_res_c"]),
                                 (g_init[:], a["g_init_row"].partition_broadcast(T))):
                    sp.dma_start(dst, src).then_inc(loads, 16)
                sp.wait_ge(cleared, 1)
                for k in range(U):
                    sp.dma_start(u[T:T + 1, k, :], a["b_in_row"]).then_inc(bias_in, 16)
                load_x(w, sp)
                for g in range(NG):
                    rows_ = a["ctx"][g * GB:(g + 1) * GB, 0:T, :].rearrange("b t d -> t b d")
                    sp.dma_start(ctx_u[:, g * GB:(g + 1) * GB, :], rows_[:, :, 0:D]).then_inc(ctx_u_in[g], 16)
                    if g >= 2:
                        sp.wait_ge(squared, nth(2 * GB * (g - 1) - 1))
                    sp.dma_start(ctx_v[:, g % 2, :, :], rows_[:, :, D:2 * D]).then_inc(ctx_v_in[g % 2], 16)

            @block.gpsimd
            def _(pool):
                nc.gpsimd.memset(zero[:], 0.0)
                nc.gpsimd.memset(ones16[:], 1.0)
                nc.gpsimd.memset(m_scan[:], 1.0)
                nc.gpsimd.memset(u[:], 0.0).then_inc(cleared, 1)
                nc.gpsimd.memset(keep[:], 1.0).then_inc(cleared, 1)
                pool.wait_ge(cleared, 2)
                nc.gpsimd.memset(keep[:, :, 0:1], 0.0).then_inc(cleared, 1)

            @block.vector
            def _(dve):
                chain = Chain(dve, chain_s)
                for s in (xn_done, u_done, x_done):
                    dve.sem_inc(s, CREDIT)

                def x_statistics(groups):
                    for g in groups:
                        dve.wait_ge(w.x_in[g], 16)
                        for r in range(GB):
                            last = nc.vector.bn_stats(stats[:, g * GB + r, :], w.x_res[:, g * GB + r, :])
                        chain.link(last)
                        for r in range(GB):
                            last = nc.vector.bn_aggr(w.mean_var[:, g * GB + r, :], stats[:, g * GB + r, :])
                    chain.link(last)

                dve.wait_ge(mask_in, 16)
                chain.link(nc.vector.tensor_copy(mask_f[:], mask_i[:]))
                dve.wait_ge(cleared, 1)
                chain.link(nc.vector.tensor_tensor_scan(cum[:], mask_f[:], zero[:], 0.0, ALU.add, ALU.add))
                nc.vector.tensor_scalar(wrap[:], cum[:], 1.0, float(T), ALU.is_lt, ALU.mult)
                chain.link(nc.vector.tensor_scalar(idx[:], cum[:], -1.0, None, ALU.add))
                nc.vector.tensor_tensor(idx[:], idx[:], wrap[:], ALU.add).then_inc(idx_done, 1)
                dve.wait_ge(loads, 16 * 4)
                for kk in range(KD):
                    chain.link(nc.vector.tensor_scalar(w_in[:, kk, :], w_in[:, kk, :], g_res[:, kk:kk + 1],
                                                       w.gates[:, 0:1], ALU.mult, ALU.mult))
                chain.link(nc.vector.tensor_scalar(g_init[:], g_init[:], w.gates[0:T, 0:1],
                                                   bcoef, ALU.mult, ALU.mult))
                dve.wait_ge(idx_tr, 1)
                chain.link(nc.vector.tensor_copy(idx_t[:], w.bank(0, CHUNK, NQ * B)))
                nc.vector.tensor_tensor(
                    hit[:], iota[0:CHUNK, 0:T].unsqueeze(1).broadcast_to([CHUNK, NQ * B, T]),
                    idx_t[:].unsqueeze(2).broadcast_to([CHUNK, NQ * B, T]), ALU.is_equal).then_inc(hit_done, 1)
                x_statistics(range(0, NG // 2))
                dve.wait_ge(counted, 1)
                for g in range(NG):
                    last = nc.vector.tensor_scalar(mark[:, g * GT:(g + 1) * GT], w.bank(g, T, GT), 1.0, None, ALU.min)
                chain.link(last)
                dve.wait_ge(cleared, 3)
                chain.link(nc.vector.tensor_tensor_scan(plug[:], keep[:].rearrange("p b t -> p (b t)"), mark[:],
                                                        0.0, ALU.mult, ALU.add))
                chain.link(nc.vector.tensor_scalar(pos[:], plug[:], -1.0, 0.0, ALU.add, ALU.max))
                chain.link(nc.vector.tensor_scalar(pos[:], pos[:], iota[0:T, T:T + 1], -dt, ALU.subtract, ALU.mult))
                nc.vector.scalar_tensor_tensor(out=expo[:], in0=pos[:], scalar=-1000.0 / dt, in1=pos[:],
                                               op0=ALU.mult, op1=ALU.min).then_inc(expo_done, 1)
                x_statistics(range(NG // 2, NG))
                dve.wait_ge(bias_in, 16 * U)
                chain.link(nc.vector.tensor_scalar(u[96:T + 1, :, :], u[96:T + 1, :, :],
                                                   w.gates[96:T + 1, 0:1], None, ALU.mult))
                dve.wait_ge(squared, nth(2 * B - 1))
                chain.link(nc.vector.tensor_tensor(ms[:, 0, :], halves[:, 0, :], halves[:, 1, :], ALU.add))
                chain.link(nc.vector.tensor_scalar(ms[:, 0, :], ms[:, 0, :], 1.0 / DC, EPS, ALU.mult, ALU.add))
                nc.vector.tensor_scalar(ms[:, 1, :], w.mean_var[:, :, 1], 1 + EPS, EPS * EPS, ALU.mult,
                                        ALU.add).then_inc(ms_done, 1)
                dve.wait_ge(root_done, 1)
                chain.link(inverse_root(nc, chain, inv[:, :, :, 0], root[:], ms[:], tmp[:]))
                for g in range(NG):
                    dve.wait_ge(ctx_u_in[g], 16)

                def front(b, r):
                    dve.wait_ge(x_tr, nth(b - U))
                    nc.vector.tensor_scalar(xn[:, r, :], w.x_res[:, b, :], w.mean_var[:, b, 0:1], inv[:, 1, b, :],
                                            ALU.subtract, ALU.mult).then_inc(xn_done, 1)
                    dve.wait_ge(y_done, nth(b - U))
                    nc.vector.scalar_tensor_tensor(out=u[0:T, r, :], in0=ctx_u[:, b, :], scalar=inv[:, 0, b, :],
                                                   in1=g_init[:], op0=ALU.mult, op1=ALU.mult).then_inc(u_done, 1)

                def back(b, r):
                    dve.wait_ge(y_done, nth(b))
                    nc.vector.tensor_tensor(w.x_res[:, b, :], w.bank(4 + r, T, D), w.x_res[:, b, :],
                                            ALU.add).then_inc(x_done, 1)
                    dve.wait_ge(x_done, nth(b))
                    alone(w, dve)
                    return nc.vector.bn_stats(stats[:, r, :], w.x_res[:, b, :])

                def next_statistics(i, last):
                    chain.link(last)
                    alone(w, dve)
                    for r in range(U):
                        last = nc.vector.bn_aggr(x_mv[:, r, :], stats[:, r, :])
                    chain.link(last)
                    alone(w, dve)
                    chain.link(nc.vector.tensor_copy(w.mean_var[:, bass.ds(U * i, U), :], x_mv[:]))

                def body(i):
                    for r in range(U):
                        front(U * i + r + 2, (r + 2) % U)
                        last = back(U * i + r, r)
                    next_statistics(i, last)
                for b in range(2):
                    front(b, b)
                chain.loop(B // U - 1, 3, body)
                for r in range(U):
                    if r < U - 2:
                        front(B - U + r + 2, r + 2)
                    last = back(B - U + r, r)
                next_statistics(B // U - 1, last)

            @block.scalar
            def _(act):
                for s in (x_t_done, m_done, squared):
                    act.sem_inc(s, CREDIT)
                n = 0
                for b in range(B):
                    g = b // GB
                    if b % GB == 0:
                        act.wait_ge(ctx_u_in[g], 16)
                        act.wait_ge(ctx_v_in[g % 2], 16 * (g // 2 + 1))
                    for h, half in enumerate((ctx_u[:, b, :], ctx_v[:, g % 2, b % GB, :])):
                        if n >= 2:
                            act.wait_ge(squared, nth(n - 2))
                        nc.scalar.activation(squares[:, n % 2, :], half, ACT.Square,
                                             accum_out=halves[:, h, b:b + 1]).then_inc(squared, 1)
                        n += 1
                act.wait_ge(ms_done, 1)
                nc.scalar.activation(root[:], ms[:], ACT.Sqrt).then_inc(root_done, 1)
                act.wait_ge(expo_done, 1)
                nc.scalar.activation(table[:], w.gates[:, 0:1], ACT.Exp)
                with act.Fori(0, B // U) as i:
                    for r in range(U):
                        b = U * i + r
                        act.wait_ge(y_done, nth(b - U))
                        nc.scalar.activation(m_scan[0:T, r, :], expo[:, bass.ds(b * T, T)], ACT.Exp).then_inc(m_done, 1)
                        act.wait_ge(x_tr, nth(b))
                        nc.scalar.activation(x_t[:, r, :, :], w.bank(r, P, KD * T).rearrange("p (k t) -> p k t", k=KD),
                                             ACT.Copy).then_inc(x_t_done, 1)

            @block.tensor
            def _(pe):
                for s in (x_tr, y_done):
                    pe.sem_inc(s, CREDIT)
                pe.wait_ge(idx_done, 1)
                for c in range(NQ):
                    last = nc.tensor.transpose(w.bank(0, CHUNK)[:, c * B:(c + 1) * B],
                                               idx[:, c * CHUNK:(c + 1) * CHUNK], w.ident[0:B, 0:B])
                last.then_inc(idx_tr, 1)
                pe.wait_ge(hit_done, 1)
                for g in range(NG):
                    for c in range(NQ):
                        last = nc.tensor.matmul(w.bank(g, T, GT), ones16[:], hit[:, c * B + g * GB:c * B + (g + 1) * GB, :],
                                                start=(c == 0), stop=(c == NQ - 1))
                last.then_inc(counted, 1)
                pe.wait_ge(expo_done, 1)

                def turn(b, r):
                    pe.wait_ge(xn_done, nth(b))
                    pe.wait_ge(x_t_done, nth(b - U))
                    for kk in range(KD):
                        last = nc.tensor.transpose(w.bank(r)[:, kk * T:(kk + 1) * T],
                                                   xn[:, r, kk * P:(kk + 1) * P], w.ident[0:T, 0:T])
                    last.then_inc(x_tr, 1)

                def product(b, r):
                    y = w.bank(4 + r, T, D)
                    pe.wait_ge(x_t_done, nth(b))
                    pe.wait_ge(x_done, nth(b - U))
                    for kk in range(KD):
                        nc.tensor.matmul(y, x_t[:, r, kk, :], w_in[:, kk, :], start=(kk == 0), stop=False)
                    pe.wait_ge(m_done, nth(b))
                    pe.wait_ge(u_done, nth(b))
                    nc.tensor.matmul(y, m_scan[0:T + 1, r, :], u[0:T + 1, r, :], start=False, stop=True).then_inc(y_done, 1)

                turn(0, 0)
                with pe.Fori(0, B // U - 1) as i:
                    for r in range(U):
                        turn(U * i + r + 1, (r + 1) % U)
                        product(U * i + r, r)
                for r in range(U):
                    if r < U - 1:
                        turn(B - U + r + 1, r + 1)
                    product(B - U + r, r)


def stage2(w):
    nc, a = w.nc, w.a
    NM1, NM2 = KD * (P // ER), D // ER
    NM = NM1 + NM2
    PAIRS = B // 2
    with ExitStack() as ctx:
        sb = lambda n, s, d=F32: ctx.enter_context(nc.sbuf_tensor(n, s, d))
        sem = w.sem
        x_t = sb("s2_x_t", [P, KD, B * T])
        xn = sb("s2_xn", [T, GB, D])
        gate1 = sb("s2_gate1", [P, KD, D])
        gate1_b = sb("s2_gate1_b", [P, KD])
        gate2 = sb("s2_gate2", [P, KD, E])
        gate2_rep = sb("s2_gate2_rep", [P, KD, P])
        gate2_b = sb("s2_gate2_b", [E, 1])
        gate2_rep_b = sb("s2_gate2_rep_b", [P, 1])
        same_row = sb("s2_same_row", [P, ER])
        tb1 = sb("s2_tb1", [E + 1, F])
        tb2 = sb("s2_tb2", [E + 1, D])
        tmp = sb("s2_tmp", [T, B])
        root = sb("s2_root", [T, B])
        var = sb("s2_var", [T, B])
        hid = sb("s2_hid", [P, 2, GT])
        hid_sum = sb("s2_hid_sum", [P, KD, B])
        gate_er = sb("s2_gate_er", [P, B])
        stats = sb("s2_stats", [T, B, 6])
        gate_1 = sb("s2_gate_1", [E + 1, B])
        gate_sel = sb("s2_gate_sel", [P, B, ER])
        bias1 = sb("s2_bias1", [P, FC, B, 1])
        tw1 = sb("s2_tw1", [P, P // ER, D])
        tw2 = sb("s2_tw2", [P, D // ER, P])
        base1 = sb("s2_base1", [P, KD, P])
        base2 = sb("s2_base2", [P, D])
        m1 = sb("s2_m1", [P, KD, B, P])
        m2 = sb("s2_m2", [P, B, D])
        act_t = sb("s2_act_t", [P, B, T])
        gate_1t = act_t[0:E + 1, :, :]

        loads = sem("s2_loads")
        tw1_in, tw2_in = sem("s2_tw1_in"), sem("s2_tw2_in")
        names = ("var_done", "root_done", "xn_done", "x_tr", "x_t_done", "hid_ps", "hid_done", "hid_sum_done",
                 "gate_ps", "gate_done", "gate_1t_done", "bias1_ps", "bias2_ps", "bias2_added", "merge_ps", "merged",
                 "h_ps", "act_done", "y_ps", "x_done", "chain", "sel_done", "bias1_done")
        S = {n: sem("s2_" + n) for n in names}

        pairs = [(gate1, "gate1_t"), (gate1_b, "gate1_b"), (gate2, "gate2_t"), (gate2_rep, "gate2_rep_t"),
                 (gate2_b, "gate2_b"), (gate2_rep_b, "gate2_rep_b"), (same_row, "same_row"), (tb1, "tb1"),
                 (tb2, "tb2")]
        N_LOADS = 16 * len(pairs)

        with nc.Block() as block:
            @block.sync
            def _(sp):
                for dst, name in pairs:
                    sp.dma_start(dst[:], a[name]).then_inc(loads, 16)

                def load(c, first):
                    if not first:
                        sp.wait_ge(S["merged"], nth(NM * (c - 1) + NM1 - 1))
                    sp.dma_start(tw1[:], a["tw1"][c]).then_inc(tw1_in, 16)
                    sp.dma_start(base1[:], a["w1_t"][c]).then_inc(tw1_in, 16)
                    if not first:
                        sp.wait_ge(S["merged"], nth(NM * (c - 1) + NM - 1))
                    sp.dma_start(tw2[:], a["tw2"][c]).then_inc(tw2_in, 16)
                    sp.dma_start(base2[:], a["w2_t"][c]).then_inc(tw2_in, 16)

                load(0, True)
                load_attention(w, sp)
                with sp.Fori(1, FC) as c:
                    load(c, False)

            @block.vector
            def _(dve):
                chain = Chain(dve, S["chain"])
                for n in ("xn_done", "hid_sum_done", "bias2_added", "merged", "x_done"):
                    dve.sem_inc(S[n], CREDIT)
                chain.link(nc.vector.memset(gate_1[:], 1.0))
                nc.vector.tensor_scalar(var[:], w.mean_var[:, :, 1], EPS, None, ALU.add).then_inc(S["var_done"], 1)
                dve.wait_ge(S["root_done"], 1)
                chain.link(inverse_root(nc, chain, w.rstd[:, :, 0], root[:], var[:], tmp[:]))

                def norm(i):
                    for r in range(GB):
                        b = GB * i + r
                        dve.wait_ge(S["x_tr"], nth(b - GB))
                        normalised(nc, w, xn[:, r, :], b).then_inc(S["xn_done"], 1)

                def sums(i):
                    for o in range(KD):
                        dve.wait_ge(S["hid_done"], nth(KD * i + o))
                        nc.vector.tensor_reduce(hid_sum[:, o, bass.ds(i * GB, GB)],
                                                hid[:, o, :].rearrange("p (b t) -> p b t", b=GB), AX.X,
                                                ALU.add).then_inc(S["hid_sum_done"], 1)

                def prepare(i):
                    norm(i + 1)
                    sums(i)

                norm(0)
                chain.loop(NG - 1, 0, prepare)
                sums(NG - 1)
                dve.wait_ge(S["gate_done"], 2)
                chain.link(nc.vector.tensor_copy(gate_1t, gate_1[:].unsqueeze(2).broadcast_to([E + 1, B, T])))
                dve.sem_inc(S["gate_1t_done"], 1)
                nc.vector.tensor_tensor(gate_sel[:], gate_er[:].unsqueeze(2).broadcast_to([P, B, ER]),
                                        same_row[:].unsqueeze(1).broadcast_to([P, B, ER]), ALU.mult).then_inc(S["sel_done"], 1)
                dve.wait_ge(S["bias1_ps"], 1)
                nc.vector.tensor_copy(bias1[:].rearrange("p c b o -> p (c b o)"),
                                      w.bank(5, P, FC * B)).then_inc(S["bias1_done"], 1)
                for p in range(PAIRS):
                    dve.wait_ge(S["bias2_ps"], p + 1)
                    nc.vector.scalar_tensor_tensor(out=w.x_res[:, 2 * p:2 * p + 2, :],
                                                   in0=w.bank(6 + p % 2, T).rearrange("t (b d) -> t b d", b=2),
                                                   scalar=w.gates[0:T, 2:3], in1=w.x_res[:, 2 * p:2 * p + 2, :],
                                                   op0=ALU.mult, op1=ALU.add).then_inc(S["bias2_added"], 1)

                def chunk(c, then=lambda p: None):
                    dve.wait_ge(tw1_in, 32 * (c + 1))
                    for n in range(NM):
                        if n == NM1:
                            dve.wait_ge(tw2_in, 32 * (c + 1))
                        dve.wait_ge(S["merge_ps"], nth(NM * c + n))
                        got = w.bank(n % 4).rearrange("p (b r) -> p b r", b=B)
                        if n < NM1:
                            q, kk = n // KD, n % KD
                            dst = m1[:, kk, :, q * ER:(q + 1) * ER]
                            base = base1[:, kk, q * ER:(q + 1) * ER]
                        else:
                            q = n - NM1
                            dst = m2[:, :, q * ER:(q + 1) * ER]
                            base = base2[:, q * ER:(q + 1) * ER]
                        nc.vector.tensor_tensor(dst, got, base.unsqueeze(1).broadcast_to([P, B, ER]),
                                                ALU.add).then_inc(S["merged"], 1)
                    for p in range(PAIRS):
                        dve.wait_ge(S["y_ps"], nth(PAIRS * c + p))
                        nc.vector.scalar_tensor_tensor(out=w.x_res[:, 2 * p:2 * p + 2, :],
                                                       in0=w.bank(6 + p % 2, T).rearrange("t (b d) -> t b d", b=2),
                                                       scalar=w.gates[0:T, 2:3], in1=w.x_res[:, 2 * p:2 * p + 2, :],
                                                       op0=ALU.mult, op1=ALU.add).then_inc(S["x_done"], 1)
                        if p:
                            then(p - 1)
                    then(PAIRS - 1)

                def pair_statistics(p):
                    dve.wait_ge(S["x_done"], nth(PAIRS * (FC - 1) + p))
                    for b in (2 * p, 2 * p + 1):
                        last = nc.vector.bn_stats(stats[:, b, :], w.x_res[:, b, :])
                    chain.link(last)
                    for b in (2 * p, 2 * p + 1):
                        last = nc.vector.bn_aggr(w.mean_var[:, b, :], stats[:, b, :])

                chain.loop(FC - 1, 0, chunk)
                chunk(FC - 1, pair_statistics)

            @block.scalar
            def _(act):
                for n in ("x_t_done", "hid_done", "act_done"):
                    act.sem_inc(S[n], CREDIT)
                act.wait_ge(S["var_done"], 1)
                nc.scalar.activation(root[:], var[:], ACT.Sqrt).then_inc(S["root_done"], 1)
                act.wait_ge(loads, N_LOADS)

                def evacuate(i):
                    for r in range(GB):
                        b = GB * i + r
                        act.wait_ge(S["x_tr"], nth(b))
                        nc.scalar.activation(x_t[:, :, bass.ds(b * T, T)],
                                             w.bank(4 + r, P, KD * T).rearrange("p (k t) -> p k t", k=KD),
                                             ACT.Copy).then_inc(S["x_t_done"], 1)

                def hidden(i):
                    for o in range(KD):
                        act.wait_ge(S["hid_ps"], nth(KD * i + o))
                        act.wait_ge(S["hid_sum_done"], nth(KD * (i - 1) + o))
                        nc.scalar.activation(hid[:, o, :], w.bank(2 + o, P, GT), ACT.Relu,
                                             bias=gate1_b[:, o:o + 1]).then_inc(S["hid_done"], 1)

                evacuate(0)
                with act.Fori(0, NG - 1) as i:
                    evacuate(i + 1)
                    hidden(i)
                hidden(NG - 1)
                act.wait_ge(S["gate_ps"], 1)
                nc.scalar.activation(gate_er[:], w.bank(4, P, B), ACT.Identity, bias=gate2_rep_b[:],
                                     scale=1.0 / T).then_inc(S["gate_done"], 1)
                nc.scalar.activation(gate_1[0:E, :], w.bank(4)[0:E, B:2 * B], ACT.Identity, bias=gate2_b[:],
                                     scale=1.0 / T).then_inc(S["gate_done"], 1)
                act.wait_ge(S["bias1_done"], 1)
                with act.Fori(0, FC) as c:
                    for g in range(NG):
                        act.wait_ge(S["h_ps"], nth(NG * c + g))
                        for r in range(GB):
                            b = GB * g + r
                            last = nc.scalar.activation(act_t[:, b, :], w.bank(4 + g % 2)[:, r * T:(r + 1) * T],
                                                        ACT.Gelu_apprx_tanh, bias=bias1[:, c, b, :])
                        last.then_inc(S["act_done"], 1)

            @block.tensor
            def _(pe):
                for n in ("x_tr", "hid_ps", "merge_ps", "h_ps", "y_ps"):
                    pe.sem_inc(S[n], CREDIT)
                pe.wait_ge(loads, N_LOADS)

                def turn_x(i):
                    for r in range(GB):
                        b = GB * i + r
                        pe.wait_ge(S["xn_done"], nth(b))
                        pe.wait_ge(S["x_t_done"], nth(b - GB))
                        for kk in range(KD):
                            last = nc.tensor.transpose(w.bank(4 + r)[:, kk * T:(kk + 1) * T],
                                                       xn[:, r, kk * P:(kk + 1) * P], w.ident[0:T, 0:T])
                        last.then_inc(S["x_tr"], 1)

                def hidden(i):
                    pe.wait_ge(S["x_t_done"], nth(GB * i + GB - 1))
                    for o in range(KD):
                        pe.wait_ge(S["hid_done"], nth(KD * (i - 1) + o))
                        for kk in range(KD):
                            last = nc.tensor.matmul(w.bank(2 + o, P, GT), gate1[:, kk, o * P:(o + 1) * P],
                                                    x_t[:, kk, bass.ds(i * GT, GT)], start=(kk == 0), stop=(kk == KD - 1))
                        last.then_inc(S["hid_ps"], 1)

                turn_x(0)
                with pe.Fori(0, NG - 1) as i:
                    turn_x(i + 1)
                    hidden(i)
                hidden(NG - 1)
                pe.wait_ge(S["hid_sum_done"], nth(KD * NG - 1))
                for kk in range(KD):
                    nc.tensor.matmul(w.bank(4, P, B), gate2_rep[:, kk, :], hid_sum[:, kk, :],
                                     start=(kk == 0), stop=(kk == KD - 1))
                for kk in range(KD):
                    last = nc.tensor.matmul(w.bank(4)[0:E, B:2 * B], gate2[:, kk, :], hid_sum[:, kk, :],
                                            start=(kk == 0), stop=(kk == KD - 1))
                last.then_inc(S["gate_ps"], 1)
                pe.wait_ge(S["gate_done"], 2)
                for c in range(FC):
                    last = nc.tensor.matmul(w.bank(5)[:, c * B:(c + 1) * B], tb1[:, c * P:(c + 1) * P], gate_1[:],
                                            start=True, stop=True)
                last.then_inc(S["bias1_ps"], 1)
                pe.wait_ge(S["gate_1t_done"], 1)
                for b in range(B):
                    p = b // 2
                    if b % 2 == 0 and p >= 2:
                        pe.wait_ge(S["bias2_added"], nth(p - 2))
                    last = nc.tensor.matmul(w.bank(6 + p % 2, T)[:, (b % 2) * D:(b % 2 + 1) * D], gate_1t[:, b, :], tb2[:],
                                            start=True, stop=True)
                    if b % 2:
                        last.then_inc(S["bias2_ps"], 1)
                pe.wait_ge(S["sel_done"], 1)
                pe.wait_ge(S["bias2_added"], nth(PAIRS - 1))
                sel = gate_sel[:].rearrange("p b r -> p (b r)")
                with pe.Fori(0, FC) as c:
                    for n in range(NM):
                        if n == 0:
                            pe.wait_ge(tw1_in, 32 * (c + 1))
                        if n == NM1:
                            pe.wait_ge(tw2_in, 32 * (c + 1))
                        pe.wait_ge(S["merged"], nth(NM * c + n - 4))
                        rows_ = tw1[:, n // KD, (n % KD) * P:(n % KD + 1) * P] if n < NM1 else tw2[:, n - NM1, :]
                        nc.tensor.matmul(w.bank(n % 4), rows_, sel, start=True, stop=True).then_inc(S["merge_ps"], 1)
                    pe.wait_ge(S["merged"], nth(NM * c + NM1 - 1))
                    for g in range(NG):
                        pe.wait_ge(S["act_done"], nth(NG * c + g - 2))
                        for r in range(GB):
                            b = GB * g + r
                            for kk in range(KD):
                                last = nc.tensor.matmul(w.bank(4 + g % 2)[:, r * T:(r + 1) * T], m1[:, kk, b, :],
                                                        x_t[:, kk, b * T:(b + 1) * T], start=(kk == 0), stop=(kk == KD - 1))
                        last.then_inc(S["h_ps"], 1)
                    pe.wait_ge(S["merged"], nth(NM * c + NM - 1))
                    for p in range(PAIRS):
                        pe.wait_ge(S["act_done"], nth(NG * c + p // 2))
                        pe.wait_ge(S["x_done"], nth(PAIRS * c + p - 2))
                        for r in range(2):
                            b = 2 * p + r
                            last = nc.tensor.matmul(w.bank(6 + p % 2, T)[:, r * D:(r + 1) * D], act_t[:, b, :], m2[:, b, :],
                                                    start=True, stop=True)
                        last.then_inc(S["y_ps"], 1)


def stage4_inputs(w):
    sb = lambda n, s, d=F32: w.ctx.enter_context(w.nc.sbuf_tensor(n, s, d))
    w.columns = {"col_emb": sb("s4_col_emb", [C4, D]), "cgate1": sb("s4_cgate1", [P, KD, P]),
                 "cgate1_b": sb("s4_cgate1_b", [P, 1]), "cgate2": sb("s4_cgate2", [P, C4]),
                 "cgate2_b": sb("s4_cgate2_b", [T, C4]), "w_cols": sb("s4_w_cols", [P, KD, F4]),
                 "b_cols": sb("s4_b_cols", [P, J4]), "proj": sb("s4_proj", [P, J4, D]),
                 "proj_b": sb("s4_proj_b", [T, D]), "ln_g": sb("s4_ln_g", [T, D]), "ln_b": sb("s4_ln_b", [T, D]),
                 "col_of": sb("s4_col_of", [3 * C4, F4]), "col_less": sb("s4_col_less", [P, C4])}
    w.columns_in = w.sem("columns_in")


def load_columns(w, sp):
    for name, dst in w.columns.items():
        src = w.a[name]
        if name in ("cgate2_b", "proj_b", "ln_g", "ln_b"):
            src = src.partition_broadcast(T)
        sp.dma_start(dst[:], src).then_inc(w.columns_in, 16)


def stage3(w):
    nc, a = w.nc, w.a
    TILE = HS * T
    K_OF = [CHUNK] * (NC - 1) + [T]
    HALVES = NC // 2
    NX = NT * HALVES
    NMX = H // 2
    MISC, OUT = 7, 6
    stage4_inputs(w)
    with ExitStack() as ctx:
        sb = lambda n, s, d=F32: ctx.enter_context(nc.sbuf_tensor(n, s, d))
        sem = w.sem
        wq, wk, wv, w_proj, shift_rows = (w.attention[n] for n in ("wq_t", "wk_t", "wv_t", "w_proj_t", "shift_rows"))
        xn = sb("s3_xn", [T, D])
        x_t = sb("s3_x_t", [P, KD, T])
        q_t = [sb(f"s3_q_t{k}", [P, NT, T]) for k in range(2)]
        q16 = sb("s3_q16", [P, NT, HS, T], BF16)
        q_m = sb("s3_q_m", [P, NT, HS, T])
        k_t = [sb(f"s3_k_t{k}", [P, NT, KPAD]) for k in range(2)]
        k16 = sb("s3_k16", [P, NT, NKEY], BF16)
        v_raw = [sb(f"s3_v_raw{k}", [CHUNK, NC - 1, D]) for k in range(2)]
        v = [sb(f"s3_v{k}", [CHUNK, NC, H, SLOT]) for k in range(2)]
        prob = [sb(f"s3_prob{k}", [CHUNK, NC, TILE]) for k in range(2)]
        neg_max = sb("s3_neg_max", [T, NT, HS, SLOT], BF16)
        ident16 = sb("s3_ident16", [T, T], BF16)
        o_t = [sb(f"s3_o_t{k}", [P, NT * T]) for k in range(2)]
        o_n = sb("s3_o_n", [P, NT * T])
        inv_den = sb("s3_inv_den", [T, H])
        inv_rep = sb("s3_inv_rep", [T, H, SLOT])
        stats, x_mv = sb("s3_stats", [T, 6]), sb("s3_x_mv", [T, 2])
        tmp, root, var = sb("s3_tmp", [T, B]), sb("s3_root", [T, B]), sb("s3_var", [T, B])

        keys_cleared, values_cleared = sem("s3_keys_cleared"), sem("s3_values_cleared")
        k_in = [sem(f"s3_k_in{k}") for k in range(2)]
        v_in = [sem(f"s3_v_in{k}") for k in range(2)]
        names = ("var_done", "root_done", "chain", "xn_done", "x_tr", "x_t_done", "q_ps", "q_done", "k_ps", "k_done",
                 "v_ps", "v_done", "q16_done", "k16_done", "v_put", "s16_ps", "max_done", "max_tr", "q_m_done",
                 "s_ps", "exp_done", "o_ps", "o_t_done", "den_ps", "inv_done", "inv_tr", "o_n_done", "y_ps", "x_done")
        S = {n: sem("s3_" + n) for n in names}
        N_WEIGHTS = 16 * len(w.attention)

        def turns(eng, turn, chain=None, per=0):
            turn(0, 0, 2, False, 0)

            def two(i):
                for n in range(2):
                    turn(2 * i + 1 + n, (1 + n) % 2, 2, True, i + 1)

            if chain is None:
                with eng.Fori(0, B // 2 - 2) as i:
                    two(i)
            else:
                chain.loop(B // 2 - 2, 2 * per, two)
            turn(B - 3, 1, 2, True, B // 2 - 1)
            turn(B - 2, 0, 1, True, B // 2 - 1)
            turn(B - 1, 1, 0, True, B // 2)

        with nc.Block() as block:
            @block.sync
            def _(sp):

                def load(b, k, first):
                    if not first:
                        sp.wait_ge(S["s_ps"], nth(NX * (b - 2) + NX - 1))
                    for s in range(HS):
                        sp.dma_start(k_t[k][s * SLOT:s * SLOT + DH, :, 0:S2], a["ctx_k_t"][b, s]).then_inc(k_in[k], 16)
                    if not first:
                        sp.wait_ge(S["v_put"], nth(b - 2))
                    sp.dma_start(v_raw[k][:], a["ctx"][b, :, D:2 * D].rearrange("(c p) d -> p c d", p=CHUNK))\
                        .then_inc(v_in[k], 16)

                for k in range(2):
                    sp.wait_ge(keys_cleared, k + 1)
                    load(k, k, True)
                load_columns(w, sp)
                with sp.Fori(1, B // 2) as i:
                    for k in range(2):
                        load(2 * i + k, k, False)

            @block.gpsimd
            def _(pool):
                pool.sem_inc(S["v_put"], CREDIT)
                for k in range(2):
                    nc.gpsimd.memset(v[k][:, :, :, 0:DH], 0.0)
                    nc.gpsimd.memset(v[k][:, :, :, DH + 1:SLOT], 0.0)
                    nc.gpsimd.memset(v[k][:, :, :, DH:DH + 1], 1.0)
                nc.gpsimd.memset(q16[:], 0.0).then_inc(values_cleared, 1)
                pool.wait_ge(values_cleared, 1)

                def front(b, k, n):
                    pool.wait_ge(v_in[k], 16 * (n + 1))
                    pool.wait_ge(S["o_ps"], nth(NT * (b - 2) + NT - 1))
                    alone(w, pool)
                    nc.gpsimd.tensor_copy(v[k][:, 0:NC - 1, :, 0:DH],
                                          v_raw[k][:].rearrange("p c (h d) -> p c h d", h=H)).then_inc(S["v_put"], 1)

                front(0, 0, 0)
                front(1, 1, 0)
                with pool.Fori(1, B // 2) as i:
                    front(2 * i, 0, i)
                    front(2 * i + 1, 1, i)

            @block.scalar
            def _(act):
                for n in ("x_t_done", "q_done", "q16_done", "k16_done", "k_done", "v_done", "exp_done", "o_t_done"):
                    act.sem_inc(S[n], CREDIT)
                act.wait_ge(S["var_done"], 1)
                nc.scalar.activation(root[:], var[:], ACT.Sqrt).then_inc(S["root_done"], 1)
                act.wait_ge(w.attention_in, N_WEIGHTS)
                for k in range(2):
                    nc.scalar.activation(k_t[k][:, :, 0:NKEY], shift_rows[:, 0:1].unsqueeze(2).broadcast_to([P, NT, NKEY]),
                                         ACT.Copy).then_inc(keys_cleared, 1)
                act.wait_ge(keys_cleared, 2)
                act.wait_ge(values_cleared, 1)

                def evacuate_x(b):
                    act.wait_ge(S["x_tr"], nth(b))
                    nc.scalar.activation(x_t[:], w.bank(MISC, P, KD * T).rearrange("p (k t) -> p k t", k=KD),
                                         ACT.Copy).then_inc(S["x_t_done"], 1)

                def evacuate_q(b, k):
                    act.wait_ge(S["q_ps"], nth(b))
                    act.wait_ge(S["q_m_done"], nth(b - 2))
                    nc.scalar.activation(q_t[k][:], w.bank(0, P, NT * T).rearrange("p (n t) -> p n t", n=NT),
                                         ACT.Identity, scale=DH ** -0.5).then_inc(S["q_done"], 1)
                    act.wait_ge(S["s16_ps"], nth(NMX * (b - 1) + NMX - 1))
                    for s in range(HS):
                        rows_ = slice(s * SLOT, (s + 1) * SLOT)
                        last = nc.scalar.activation(q16[rows_, :, s, :],
                                                    w.banks[rows_, 0, 0:NT * T].rearrange("p (n t) -> p n t", n=NT),
                                                    ACT.Identity, scale=DH ** -0.5)
                    last.then_inc(S["q16_done"], 1)

                def evacuate_k(b, k):
                    act.wait_ge(S["k_ps"], nth(b))
                    got = w.bank(1, P, NT * T).rearrange("p (n t) -> p n t", n=NT)
                    nc.scalar.activation(k_t[k][:, :, S2:NKEY], got, ACT.Identity, bias=shift_rows[:, 0:1])
                    nc.scalar.activation(k16[:, :, S2:NKEY], got, ACT.Copy).then_inc(S["k_done"], 1)

                def evacuate_v(b, k):
                    act.wait_ge(S["v_ps"], nth(b))
                    nc.scalar.activation(v[k][0:T, NC - 1, :, 0:DH], w.bank(0, T, D).rearrange("p (h d) -> p h d", h=H),
                                         ACT.Copy).then_inc(S["v_done"], 1)

                def round_keys(b, k, n):
                    act.wait_ge(k_in[k], 16 * HS * (n + 1))
                    nc.scalar.activation(k16[:, :, 0:S2], k_t[k][:, :, 0:S2], ACT.Copy).then_inc(S["k16_done"], 1)

                def exp(b, t, h):
                    if h == 0:
                        act.wait_ge(S["o_ps"], nth(NT * b + t - 2))
                    act.wait_ge(S["s_ps"], nth(NX * b + HALVES * t + h))
                    nc.scalar.activation(prob[t % 2][:, 2 * h:2 * h + 2, :],
                                         w.banks[0:CHUNK, 2 + 2 * h:4 + 2 * h, 0:TILE], ACT.Exp).then_inc(S["exp_done"], 1)

                def turn(b, k, ahead, tail, used):
                    if ahead:
                        evacuate_q(b + 1, 1 - k)
                        evacuate_k(b + 1, 1 - k)
                        round_keys(b + 1, 1 - k, used)
                        evacuate_v(b + 1, 1 - k)
                    for t in range(NT):
                        if t == NT - 1 and ahead == 2:
                            evacuate_x(b + 2)
                        exp(b, t, 0)
                        exp(b, t, 1)
                    act.wait_ge(S["o_ps"], nth(NT * b + NT - 1))
                    act.wait_ge(S["o_n_done"], nth(b - 2))
                    nc.scalar.activation(o_t[k][:], w.bank(OUT, P, NT * T), ACT.Copy).then_inc(S["o_t_done"], 1)

                evacuate_x(0)
                evacuate_q(0, 0)
                evacuate_k(0, 0)
                evacuate_v(0, 0)
                round_keys(0, 0, 0)
                evacuate_x(1)
                turns(act, turn)

            @block.vector
            def _(dve):
                chain = Chain(dve, S["chain"])
                for n in ("xn_done", "max_done", "q_m_done", "inv_done", "o_n_done", "x_done"):
                    dve.sem_inc(S[n], CREDIT)
                nc.vector.tensor_scalar(var[:], w.mean_var[:, :, 1], EPS, None, ALU.add).then_inc(S["var_done"], 1)
                nc.vector.memset(neg_max[:], 0.0)
                nc.vector.tensor_copy(ident16[:], w.ident[0:T, 0:T])
                for k in range(2):
                    nc.vector.memset(k_t[k][:, :, NKEY:KPAD], 0.0)
                chain.link(nc.vector.memset(q_m[:], 0.0))
                dve.wait_ge(S["root_done"], 1)
                chain.link(inverse_root(nc, chain, w.rstd[:, :, 0], root[:], var[:], tmp[:]))

                def norm(b):
                    dve.wait_ge(S["x_tr"], nth(b - 1))
                    normalised(nc, w, xn[:], b).then_inc(S["xn_done"], 1)

                def maximum(b, j, ring=1):
                    if j == 0:
                        dve.wait_ge(S["max_tr"], nth(b - 1))
                    dve.wait_ge(S["s16_ps"], nth(NMX * b + j))
                    t, s = divmod(2 * j, HS)
                    nc.vector.tensor_reduce(neg_max[:, t, s:s + 2, DH:DH + 1], w.banks[0:T, 2 * (j % ring):2 * (j % ring) + 2, 0:NKEY], AX.X, ALU.max,
                                            negate=True).then_inc(S["max_done"], 1)

                def place_queries(b, k):
                    dve.wait_ge(S["max_tr"], nth(b))
                    for s in range(HS):
                        rows_ = slice(s * SLOT, (s + 1) * SLOT)
                        last = nc.vector.tensor_tensor(q_m[rows_, :, s, :],
                                                       w.banks[rows_, MISC, 0:NT * T].rearrange("p (n t) -> p n t", n=NT),
                                                       q_t[k][rows_, :, :], ALU.add)
                    last.then_inc(S["q_m_done"], 1)

                def invert(b):
                    dve.wait_ge(S["den_ps"], nth(b))
                    dve.wait_ge(S["inv_tr"], nth(b - 1))
                    chain.link(nc.vector.reciprocal(inv_den[:], w.bank(MISC, T, H)))
                    nc.vector.tensor_copy(inv_rep[:], inv_den[:].unsqueeze(2).broadcast_to([T, H, SLOT]))\
                        .then_inc(S["inv_done"], 1)

                def weigh(b, k):
                    dve.wait_ge(S["inv_tr"], nth(b))
                    nc.vector.tensor_tensor(o_n[:], o_t[k][:], w.bank(MISC, P, NT * T), ALU.mult).then_inc(S["o_n_done"], 1)

                def add(b):
                    dve.wait_ge(S["y_ps"], nth(b))
                    chain.link(nc.vector.scalar_tensor_tensor(out=w.x_res[:, b, :], in0=w.bank(MISC, T, D),
                                                              scalar=w.gates[0:T, 1:2], in1=w.x_res[:, b, :],
                                                              op0=ALU.mult, op1=ALU.add))
                    chain.link(statistics(nc, w, chain, stats[:], x_mv[:], w.x_res[:, b, :]))
                    alone(w, dve)
                    nc.vector.tensor_copy(w.mean_var[:, b, :], x_mv[:]).then_inc(S["x_done"], 1)

                def turn(b, k, ahead, tail, used):
                    place_queries(b, k)
                    if ahead == 2:
                        norm(b + 2)
                    for j in range(NMX):
                        if tail and j == 0:
                            invert(b - 1)
                        if tail and j == 1:
                            weigh(b - 1, 1 - k)
                        if tail and j == 3:
                            add(b - 1)
                        if ahead:
                            maximum(b + 1, j)

                norm(0)
                norm(1)
                for j in range(NMX):
                    maximum(0, j, 3)
                turns(dve, turn, chain, 4)
                invert(B - 1)
                weigh(B - 1, 1)
                add(B - 1)

            @block.tensor
            def _(pe):
                for n in ("x_tr", "q_ps", "k_ps", "v_ps", "s16_ps", "max_tr", "s_ps", "o_ps", "den_ps", "inv_tr", "y_ps"):
                    pe.sem_inc(S[n], CREDIT)
                pe.wait_ge(w.attention_in, N_WEIGHTS)

                def turn_x(b):
                    pe.wait_ge(S["xn_done"], nth(b))
                    pe.wait_ge(S["x_done"], nth(b - 3))
                    pe.wait_ge(S["q_m_done"], nth(b - 2))
                    for kk in range(KD):
                        last = nc.tensor.transpose(w.bank(MISC)[:, kk * T:(kk + 1) * T], xn[:, kk * P:(kk + 1) * P],
                                                   w.ident[0:T, 0:T])
                    last.then_inc(S["x_tr"], 1)

                def project(weight, bank, signal):
                    for t in range(NT):
                        for kk in range(KD):
                            last = nc.tensor.matmul(w.bank(bank)[:, t * T:(t + 1) * T], weight[:, kk, t, :], x_t[:, kk, :],
                                                    start=(kk == 0), stop=(kk == KD - 1))
                    last.then_inc(S[signal], 1)

                def projections(b):
                    pe.wait_ge(S["x_t_done"], nth(b))
                    pe.wait_ge(S["max_done"], nth(NMX * (b - 1) + NMX - 1))
                    project(wq, 0, "q_ps")
                    project(wk, 1, "k_ps")

                def values(b):
                    pe.wait_ge(S["q16_done"], nth(b))
                    for kk in range(KD):
                        last = nc.tensor.matmul(w.bank(0, T, D), x_t[:, kk, :], wv[:, kk, :],
                                                start=(kk == 0), stop=(kk == KD - 1))
                    last.then_inc(S["v_ps"], 1)

                def rough_scores(b, j, ring=1):
                    if j == 0:
                        pe.wait_ge(S["v_done"], nth(b))
                        pe.wait_ge(S["k16_done"], nth(b))
                    pe.wait_ge(S["max_done"], nth(NMX * b + j - ring))
                    for n in range(2):
                        t, s = divmod(2 * j + n, HS)
                        last = nc.tensor.matmul(w.bank(2 * (j % ring) + n, T, NKEY), q16[:, t, s, :], k16[:, t, :], start=True, stop=True)
                    last.then_inc(S["s16_ps"], 1)

                def turn_maxima(b, ahead):
                    pe.wait_ge(S["max_done"], nth(NMX * b + NMX - 1))
                    if ahead:
                        pe.wait_ge(S["x_t_done"], nth(b + 1))
                    else:
                        pe.wait_ge(S["x_done"], nth(b - 2))
                    for t in range(NT):
                        last = nc.tensor.matmul(w.bank(MISC)[:, t * T:(t + 1) * T],
                                                neg_max[:, t, :, :].rearrange("p s e -> p (s e)"), ident16[:],
                                                start=True, stop=True)
                    last.then_inc(S["max_tr"], 1)

                def scores(b, k, t, h):
                    if t == 0 and h == 0:
                        pe.wait_ge(S["q_m_done"], nth(b))
                    pe.wait_ge(S["exp_done"], nth(NX * b + HALVES * t + h - 2))
                    for n in range(2):
                        c = 2 * h + n
                        last = nc.tensor.matmul(w.bank(2 + c, CHUNK, TILE), k_t[k][:, t, c * CHUNK:(c + 1) * CHUNK],
                                                q_m[:, t, :, :], start=True, stop=True)
                    last.then_inc(S["s_ps"], 1)

                def outputs(b, k, t):
                    if t == 0:
                        pe.wait_ge(S["o_t_done"], nth(b - 1))
                        pe.wait_ge(S["v_put"], nth(b))
                        pe.wait_ge(S["v_done"], nth(b))
                    pe.wait_ge(S["exp_done"], nth(NX * b + HALVES * t + 1))
                    for c in range(NC):
                        for s in range(HS):
                            last = nc.tensor.matmul(w.banks[s * SLOT:(s + 1) * SLOT, OUT, t * T:(t + 1) * T],
                                                    v[k][0:K_OF[c], c, t * HS + s, :],
                                                    prob[t % 2][0:K_OF[c], c, s * T:(s + 1) * T],
                                                    start=(c == 0), stop=(c == NC - 1))
                    last.then_inc(S["o_ps"], 1)

                def denominators(b, k, last_batch=False):
                    pe.wait_ge(S["o_t_done"], nth(b))
                    pe.wait_ge(S["x_done"], nth(b - 1))
                    if not last_batch:
                        pe.wait_ge(S["q_m_done"], nth(b + 1))
                    for t in range(NT):
                        last = nc.tensor.matmul(w.bank(MISC)[0:T, t * HS:(t + 1) * HS], o_t[k][:, t * T:(t + 1) * T],
                                                shift_rows[:, 1:1 + HS], start=True, stop=True)
                    last.then_inc(S["den_ps"], 1)

                def turn_inverses(b):
                    pe.wait_ge(S["inv_done"], nth(b))
                    for t in range(NT):
                        last = nc.tensor.transpose(w.bank(MISC)[:, t * T:(t + 1) * T],
                                                   inv_rep[:, t * HS:(t + 1) * HS, :].rearrange("p s e -> p (s e)"),
                                                   w.ident[0:T, 0:T])
                    last.then_inc(S["inv_tr"], 1)

                def project_out(b):
                    pe.wait_ge(S["o_n_done"], nth(b))
                    for t in range(NT):
                        last = nc.tensor.matmul(w.bank(MISC, T, D), o_n[:, t * T:(t + 1) * T], w_proj[:, t, :],
                                                start=(t == 0), stop=(t == NT - 1))
                    last.then_inc(S["y_ps"], 1)

                def turn(b, k, ahead, tail, used):
                    n = iter(range(NMX))

                    def rough():
                        if ahead:
                            rough_scores(b + 1, next(n))

                    turn_maxima(b, ahead)
                    if ahead:
                        projections(b + 1)
                    scores(b, k, 0, 0)
                    if ahead:
                        values(b + 1)
                    scores(b, k, 0, 1)
                    if tail:
                        denominators(b - 1, 1 - k)
                    rough()
                    scores(b, k, 1, 0)
                    if tail:
                        turn_inverses(b - 1)
                    rough()
                    scores(b, k, 1, 1)
                    rough()
                    if tail:
                        project_out(b - 1)
                    outputs(b, k, 0)
                    rough()
                    scores(b, k, 2, 0)
                    rough()
                    scores(b, k, 2, 1)
                    if ahead == 2:
                        turn_x(b + 2)
                    outputs(b, k, 1)
                    rough()
                    scores(b, k, 3, 0)
                    rough()
                    scores(b, k, 3, 1)
                    outputs(b, k, 2)
                    rough()
                    outputs(b, k, 3)

                turn_x(0)
                projections(0)
                values(0)
                turn_x(1)
                for j in range(NMX):
                    rough_scores(0, j, 3)
                turns(pe, turn)
                denominators(B - 1, 1, last_batch=True)
                turn_inverses(B - 1)
                project_out(B - 1)

def stage4(w):
    nc, a = w.nc, w.a
    with ExitStack() as ctx:
        sb = lambda n, s, d=F32: ctx.enter_context(nc.sbuf_tensor(n, s, d))
        sem = w.sem
        col_emb, cgate1, cgate1_b, cgate2, cgate2_b, w_cols, b_cols, proj, proj_b, ln_g, ln_b, col_of, col_less = \
            w.columns.values()
        N_COLUMNS = 16 * len(w.columns)
        xn = sb("s4_xn", [T, B, D])
        x_t = sb("s4_x_t", [P, KD, B * T])
        col_sq = sb("s4_col_sq", [C4, D])
        col_ss, col_root, col_inv = (sb("s4_col_" + n, [C4, 1]) for n in ("ss", "root", "inv"))
        col_tmp = sb("s4_col_tmp", [C4, 1])
        col_t = sb("s4_col_t", [P, KD, C4])
        col_of16 = sb("s4_col_of16", [3 * C4, F4], BF16)

        wts_t = sb("s4_wts_t", [3 * C4, B * T], BF16)
        with ExitStack() as first:
            fb = lambda n, s, d=F32: first.enter_context(nc.sbuf_tensor(n, s, d))
            tmp, root, var = fb("s4_tmp", [T, B]), fb("s4_root", [T, B]), fb("s4_var", [T, B])
            table = fb("s4_table", [P, 1])
            ident16 = fb("s4_ident16", [T, T], BF16)
            parts = fb("s4_parts", [T, B, 3, C4], BF16)
            xn_g = fb("s4_xn_g", [T, GB, D])
            x_g = [fb(f"s4_x_g{k}", [P, GB, KD, T]) for k in range(2)]
            sumsq = fb("s4_sumsq", [T, B])
            inv_norm = fb("s4_inv_norm", [T, B])
            hid = fb("s4_hid", [P, GT])
            logit, gate, eq, val = (fb("s4_" + n, [T, B, C4]) for n in ("logit", "gate", "eq", "val"))
            top, low, total = (fb("s4_" + n, [T, B]) for n in ("top", "low", "total"))
            names = ("var_done", "root_done", "chain", "xn_done", "x_tr", "x_g_done", "hid_ps", "hid_done",
                     "logit_ps", "logit_done", "ss_done", "ss_root", "logits_in", "sig_done", "diff_done", "exp_done", "wts_done", "wts_ps",
                     "col_ss_done", "col_ss_max", "col_root_done", "col_n_done", "col_ps", "col_t_done", "biased", "kept")
            S = {n: sem("s4_" + n) for n in names}
            def pairs(eng, group, chain=None):
                def two(i):
                    group(2 * i, 0, 2)
                    group(2 * i + 1, 1, 2)

                if chain is None:
                    with eng.Fori(0, NG // 2 - 1) as i:
                        two(i)
                else:
                    chain.loop(NG // 2 - 1, 0, two)
                group(NG - 2, 0, 1)
                group(NG - 1, 1, 0)

            with nc.Block() as block:
                @block.gpsimd
                def _(pool):
                    pool.wait_ge(w.columns_in, N_COLUMNS)
                    pool.wait_ge(S["biased"], 1)
                    pool.sem_inc(S["kept"], CREDIT)
                    with pool.Fori(0, NG) as i:
                        for r in range(GB):
                            b = GB * i + r
                            pool.wait_ge(S["xn_done"], nth(b))
                            nc.gpsimd.tensor_tensor(w.x_res[:, b, :], w.x_res[:, b, :], ln_b[:], ALU.add)
                            nc.gpsimd.tensor_tensor(xn[:, b, :], xn_g[:, r, :], proj_b[:], ALU.add).then_inc(S["kept"], 1)

                @block.scalar
                def _(act):
                    for n in ("x_g_done", "hid_done"):
                        act.sem_inc(S[n], CREDIT)
                    act.wait_ge(w.columns_in, N_COLUMNS)
                    nc.scalar.activation(col_sq[:], col_emb[:], ACT.Square, accum_out=col_ss[:]).then_inc(S["col_ss_done"], 1)
                    act.wait_ge(S["col_ss_max"], 1)
                    nc.scalar.activation(col_root[:], col_ss[:], ACT.Sqrt).then_inc(S["col_root_done"], 1)
                    act.wait_ge(S["var_done"], 1)
                    nc.scalar.activation(root[:], var[:], ACT.Sqrt).then_inc(S["root_done"], 1)
                    act.wait_ge(S["col_ps"], 1)
                    nc.scalar.activation(col_t[:], w.bank(4, P, KD * C4).rearrange("p (k c) -> p k c", k=KD),
                                         ACT.Copy).then_inc(S["col_t_done"], 1)

                    def evacuate(i, k):
                        act.wait_ge(S["logit_ps"], nth(i - 2))
                        for r in range(GB):
                            b = GB * i + r
                            act.wait_ge(S["x_tr"], nth(b))
                            got = w.bank(4 + r, P, KD * T).rearrange("p (k t) -> p k t", k=KD)
                            nc.scalar.activation(x_t[:, :, bass.ds(b * T, T)], got, ACT.Copy)
                            nc.scalar.activation(x_g[k][:, r, :, :], got, ACT.Copy).then_inc(S["x_g_done"], 1)

                    def hidden(i):
                        act.wait_ge(S["hid_ps"], nth(i))
                        nc.scalar.activation(hid[:], w.bank(2, P, GT), ACT.Gelu, bias=cgate1_b[:]).then_inc(S["hid_done"], 1)

                    def group(i, k, ahead):
                        if ahead:
                            evacuate(i + 1, 1 - k)
                        hidden(i)

                    act.wait_ge(S["ss_done"], 1)
                    nc.scalar.activation(root[:], sumsq[:], ACT.Sqrt).then_inc(S["ss_root"], 1)
                    nc.scalar.activation(table[:], cgate1_b[:], ACT.Gelu)
                    evacuate(0, 0)
                    pairs(act, group)
                    act.wait_ge(S["logits_in"], 1)
                    nc.scalar.activation(gate[:], gate[:], ACT.Sigmoid).then_inc(S["sig_done"], 1)
                    act.wait_ge(S["diff_done"], 1)
                    nc.scalar.activation(logit[:], logit[:], ACT.Exp).then_inc(S["exp_done"], 1)
                    act.wait_ge(S["wts_ps"], 1)
                    for g in range(0, NG, 2):
                        nc.scalar.activation(wts_t[:, g * GT:(g + 1) * GT], w.bank(g)[0:3 * C4, 0:GT], ACT.Copy)

                @block.vector
                def _(dve):
                    chain = Chain(dve, S["chain"])
                    for n in ("xn_done", "logit_done"):
                        dve.sem_inc(S[n], CREDIT)
                    nc.vector.tensor_scalar(var[:], w.mean_var[:, :, 1], EPS, None, ALU.add).then_inc(S["var_done"], 1)
                    dve.wait_ge(w.columns_in, N_COLUMNS)
                    chain.link(nc.vector.tensor_scalar(ln_g[:], ln_g[:], w.gates[0:T, 3:4], None, ALU.mult))
                    nc.vector.tensor_scalar(ln_b[:], ln_b[:], w.gates[0:T, 3:4], None, ALU.mult).then_inc(S["biased"], 1)
                    dve.wait_ge(S["col_ss_done"], 1)
                    nc.vector.tensor_scalar(col_ss[:], col_ss[:], 1e-24, None, ALU.max).then_inc(S["col_ss_max"], 1)
                    dve.wait_ge(S["col_root_done"], 1)
                    chain.link(inverse_root(nc, chain, col_inv[:], col_root[:], col_ss[:], col_tmp[:]))
                    nc.vector.tensor_scalar(col_emb[:], col_emb[:], col_inv[:], None, ALU.mult).then_inc(S["col_n_done"], 1)
                    dve.wait_ge(S["root_done"], 1)
                    chain.link(inverse_root(nc, chain, w.rstd[:, :, 0], root[:], var[:], tmp[:]))
                    chain.link(nc.vector.tensor_tensor(sumsq[:], w.rstd[:, :, 0], w.rstd[:, :, 0], ALU.mult))
                    chain.link(nc.vector.tensor_tensor(sumsq[:], sumsq[:], w.mean_var[:, :, 1], ALU.mult))
                    nc.vector.tensor_scalar(sumsq[:], sumsq[:], float(D), 1e-24, ALU.mult, ALU.max).then_inc(S["ss_done"], 1)
                    nc.vector.tensor_copy(ident16[:], w.ident[0:T, 0:T])
                    nc.vector.tensor_copy(col_of16[:], col_of[:])

                    def norm(i):
                        for r in range(GB):
                            b = GB * i + r
                            dve.wait_ge(S["x_tr"], nth(b - GB))
                            dve.wait_ge(S["kept"], nth(b - GB))
                            normalised(nc, w, xn_g[:, r, :], b).then_inc(S["xn_done"], 1)

                    def group(i, k, ahead):
                        if ahead == 2:
                            norm(i + 2)
                        dve.wait_ge(S["logit_ps"], nth(i))
                        got = w.bank(3, T, GB * 2 * C4).rearrange("p (b c) -> p b c", b=GB)
                        nc.vector.tensor_tensor(gate[:, bass.ds(i * GB, GB), :], got[:, :, 0:C4],
                                                cgate2_b[:].unsqueeze(1).broadcast_to([T, GB, C4]), ALU.add)
                        nc.vector.tensor_tensor(logit[:, bass.ds(i * GB, GB), :], got[:, :, C4:2 * C4],
                                                inv_norm[:, bass.ds(i * GB, GB)].unsqueeze(2).broadcast_to([T, GB, C4]),
                                                ALU.mult)\
                            .then_inc(S["logit_done"], 1)

                    norm(0)
                    norm(1)
                    dve.wait_ge(S["ss_root"], 1)
                    chain.link(inverse_root(nc, chain, inv_norm[:], root[:], sumsq[:], tmp[:]))
                    pairs(dve, group, chain)
                    dve.wait_ge(S["logit_done"], nth(NG - 1))
                    dve.sem_inc(S["logits_in"], 1)

                    def each(v):
                        return v[:].unsqueeze(2).broadcast_to([T, B, C4])

                    dve.wait_ge(S["sig_done"], 1)
                    chain.link(nc.vector.tensor_tensor(logit[:], logit[:], gate[:], ALU.add))
                    chain.link(nc.vector.tensor_reduce(top[:], logit[:], AX.X, ALU.max))
                    chain.link(nc.vector.tensor_tensor(eq[:], logit[:], each(top), ALU.is_equal))
                    nc.vector.tensor_tensor(logit[:], logit[:], each(top), ALU.subtract).then_inc(S["diff_done"], 1)
                    chain.link(nc.vector.tensor_tensor(val[:], eq[:], col_less[0:T, :].unsqueeze(1).broadcast_to([T, B, C4]),
                                                       ALU.mult))
                    chain.link(nc.vector.tensor_reduce(low[:], val[:], AX.X, ALU.min))
                    chain.link(nc.vector.tensor_tensor(eq[:], val[:], each(low), ALU.is_equal))
                    dve.wait_ge(S["exp_done"], 1)
                    chain.link(nc.vector.tensor_reduce(total[:], logit[:], AX.X, ALU.add))
                    chain.link(nc.vector.reciprocal(total[:], total[:]))
                    chain.link(nc.vector.tensor_tensor(val[:], logit[:], eq[:], ALU.mult))
                    chain.link(nc.vector.tensor_tensor(val[:], val[:], each(total), ALU.mult))
                    chain.link(nc.vector.tensor_copy(parts[:, :, 0, :], val[:]))
                    chain.link(nc.vector.tensor_tensor(val[:], val[:], parts[:, :, 0, :], ALU.subtract))
                    chain.link(nc.vector.tensor_copy(parts[:, :, 1, :], val[:]))
                    nc.vector.tensor_tensor(parts[:, :, 2, :], val[:], parts[:, :, 1, :], ALU.subtract)\
                        .then_inc(S["wts_done"], 1)
                    dve.wait_ge(S["wts_ps"], 1)
                    for g in range(1, NG, 2):
                        nc.vector.tensor_copy(wts_t[:, g * GT:(g + 1) * GT], w.bank(g)[0:3 * C4, 0:GT])

                @block.tensor
                def _(pe):
                    for n in ("x_tr", "hid_ps", "logit_ps"):
                        pe.sem_inc(S[n], CREDIT)
                    pe.wait_ge(S["col_n_done"], 1)
                    for kk in range(KD):
                        last = nc.tensor.transpose(w.bank(4)[:, kk * C4:(kk + 1) * C4], col_emb[:, kk * P:(kk + 1) * P],
                                                   w.ident[0:C4, 0:C4])
                    last.then_inc(S["col_ps"], 1)
                    pe.wait_ge(S["col_t_done"], 1)

                    def turn_x(i):
                        for r in range(GB):
                            b = GB * i + r
                            pe.wait_ge(S["xn_done"], nth(b))
                            pe.wait_ge(S["x_g_done"], nth(b - GB))
                            for kk in range(KD):
                                last = nc.tensor.transpose(w.bank(4 + r)[:, kk * T:(kk + 1) * T],
                                                           xn_g[:, r, kk * P:(kk + 1) * P], w.ident[0:T, 0:T])
                            last.then_inc(S["x_tr"], 1)

                    def group(i, k, ahead):
                        if ahead:
                            turn_x(i + 1)
                        pe.wait_ge(S["x_g_done"], nth(GB * i + GB - 1))
                        pe.wait_ge(S["hid_done"], nth(i - 1))
                        for kk in range(KD):
                            last = nc.tensor.matmul(w.bank(2, P, GT), cgate1[:, kk, :], x_g[k][:, :, kk, :],
                                                    start=(kk == 0), stop=(kk == KD - 1))
                        last.then_inc(S["hid_ps"], 1)
                        pe.wait_ge(S["logit_done"], nth(i - 1))
                        for r in range(GB):
                            at = r * 2 * C4
                            for kk in range(KD):
                                nc.tensor.matmul(w.bank(3, T)[:, at + C4:at + 2 * C4], x_g[k][:, r, kk, :],
                                                        col_t[:, kk, :], start=(kk == 0), stop=(kk == KD - 1))
                        pe.wait_ge(S["hid_done"], nth(i))
                        for r in range(GB):
                            at = r * 2 * C4
                            last = nc.tensor.matmul(w.bank(3, T)[:, at:at + C4], hid[:, r * T:(r + 1) * T], cgate2[:],
                                                    start=True, stop=True)
                        last.then_inc(S["logit_ps"], 1)

                    turn_x(0)
                    pairs(pe, group)
                    pe.wait_ge(S["wts_done"], 1)
                    for b in range(B):
                        last = nc.tensor.matmul(w.bank(b // GB)[0:3 * C4, (b % GB) * T:(b % GB + 1) * T],
                                                parts[:, b, :, :].rearrange("t n c -> t (n c)"), ident16[:],
                                                start=True, stop=True)
                    last.then_inc(S["wts_ps"], 1)

        hid_c = [sb(f"s4_hid_c{n}", [P, GT]) for n in range(2)]
        weighted = [sb(f"s4_weighted{n}", [P, J4, GT]) for n in range(2)]
        res = [sb(f"s4_res{n}", [T, GB, D]) for n in range(2)]
        stats = sb("s4_stats", [T, GB, 6])
        y_mv = [sb(f"s4_y_mv{n}", [T, GB, 2]) for n in range(2)]
        y_var, y_root, y_inv, y_tmp = (sb("s4_y_" + n, [T, GB]) for n in ("var", "root", "inv", "tmp"))
        names = ("col_ps", "gelu_done", "weigh_done", "y_ps", "y_done", "y_var_done", "y_root_done", "res_done", "chain2")
        S = {n: sem("s4b_" + n) for n in names}
        stored = [sem(f"s4_stored{k}") for k in range(2)]

        def turns(turn, eng=None, chain=None, per=0):
            turn(0, 0, False, 0)

            def two(i):
                turn(2 * i + 1, 1, True, i)
                turn(2 * i + 2, 0, True, i)

            if chain is None:
                with eng.Fori(0, NG // 2 - 1) as i:
                    two(i)
            else:
                chain.loop(NG // 2 - 1, 2 * per, two)
            turn(NG - 1, 1, True, NG // 2 - 1)

        with nc.Block() as block:
            @block.sync
            def _(sp):
                with sp.Fori(0, NG // 2) as i:
                    for k in range(2):
                        g = 2 * i + k
                        sp.wait_ge(S["res_done"], nth(g))
                        sp.dma_start(w.out[bass.ds(g * GB, GB)].rearrange("b t d -> t b d"), res[k][:]).then_inc(stored[k], 16)
                for k in range(2):
                    sp.wait_ge(stored[k], 16 * (NG // 2))

            @block.scalar
            def _(act):
                for n in ("gelu_done", "y_root_done"):
                    act.sem_inc(S[n], CREDIT)

                def norm_root(g):
                    act.wait_ge(S["y_var_done"], nth(g))
                    nc.scalar.activation(y_root[:], y_var[:], ACT.Sqrt).then_inc(S["y_root_done"], 1)

                def turn(g, k, tail, n):
                    for j in range(J4):
                        act.wait_ge(S["col_ps"], nth(J4 * g + j))
                        act.wait_ge(S["weigh_done"], nth(J4 * g + j - 2))
                        nc.scalar.activation(hid_c[j % 2][:], w.bank(j % 2, P, GT), ACT.Gelu,
                                             bias=b_cols[:, j:j + 1]).then_inc(S["gelu_done"], 1)
                    if tail:
                        norm_root(g - 1)

                turns(turn, act)
                norm_root(NG - 1)

            @block.vector
            def _(dve):
                chain = Chain(dve, S["chain2"])
                for n in ("weigh_done", "y_done", "y_var_done", "res_done"):
                    dve.sem_inc(S[n], CREDIT)

                def weigh(g, k, j):
                    if j == 0:
                        dve.wait_ge(S["y_ps"], nth(GB * (g - 2) + GB - 1))
                    dve.wait_ge(S["gelu_done"], nth(J4 * g + j))
                    nc.vector.tensor_tensor(weighted[k][:, j, :], hid_c[j % 2][:], w.bank(2 + j % 2, P, GT),
                                            ALU.mult).then_inc(S["weigh_done"], 1)

                def residual(g, k, r):
                    b = GB * g + r
                    dve.wait_ge(S["y_ps"], nth(b))
                    chain.link(nc.vector.tensor_tensor(xn[:, b, :], w.bank(4 + r, T, D), xn[:, b, :], ALU.add))
                    statistics(nc, w, chain, stats[:, r, :], y_mv[k][:, r, :], xn[:, b, :]).then_inc(S["y_done"], 1)

                def variance(g, k):
                    dve.wait_ge(S["y_done"], nth(GB * g + GB - 1))
                    nc.vector.tensor_scalar(y_var[:], y_mv[k][:, :, 1], EPS, None, ALU.add).then_inc(S["y_var_done"], 1)

                def finish(g, k, n):
                    dve.wait_ge(S["y_root_done"], nth(g))
                    chain.link(inverse_root(nc, chain, y_inv[:], y_root[:], y_var[:], y_tmp[:]))
                    dve.wait_ge(stored[k], 16 * n)
                    for r in range(GB):
                        last = nc.vector.tensor_scalar(res[k][:, r, :], xn[:, GB * g + r, :], y_mv[k][:, r, 0:1],
                                                       y_inv[:, r:r + 1], ALU.subtract, ALU.mult)
                    chain.link(last)
                    chain.link(nc.vector.tensor_tensor(res[k][:], res[k][:], ln_g[:].unsqueeze(1).broadcast_to([T, GB, D]),
                                                       ALU.mult))
                    nc.vector.tensor_tensor(res[k][:], res[k][:], w.x_res[:, bass.ds(GB * g, GB), :], ALU.add)\
                        .then_inc(S["res_done"], 1)

                def turn(g, k, tail, n):
                    for j in range(J4):
                        weigh(g, k, j)
                        if tail and j % 2:
                            residual(g - 1, 1 - k, j // 2)
                    if tail:
                        variance(g - 1, 1 - k)
                        finish(g - 1, 1 - k, n)

                turns(turn, None, chain, 2 * GB + 7)
                for r in range(GB):
                    residual(NG - 1, 1, r)
                variance(NG - 1, 1)
                finish(NG - 1, 1, NG // 2 - 1)

            @block.tensor
            def _(pe):
                for n in ("col_ps", "y_ps"):
                    pe.sem_inc(S[n], CREDIT)

                def columns(g, j):
                    pe.wait_ge(S["weigh_done"], nth(J4 * g + j - 2))
                    alone(w, pe)
                    nc.tensor.matmul(w.bank(2 + j % 2, P, GT), col_of16[:, j * P:(j + 1) * P], wts_t[:, bass.ds(g * GT, GT)],
                                     start=True, stop=True)
                    for kk in range(KD):
                        last = nc.tensor.matmul(w.bank(j % 2, P, GT), w_cols[:, kk, j * P:(j + 1) * P],
                                                x_t[:, kk, bass.ds(g * GT, GT)], start=(kk == 0), stop=(kk == KD - 1))
                    last.then_inc(S["col_ps"], 1)

                def output(g, k, r):
                    if r == 0:
                        pe.wait_ge(S["weigh_done"], nth(J4 * g + J4 - 1))
                    pe.wait_ge(S["y_done"], nth(GB * (g - 1) + r))
                    for j in range(J4):
                        last = nc.tensor.matmul(w.bank(4 + r, T, D), weighted[k][:, j, r * T:(r + 1) * T], proj[:, j, :],
                                                start=(j == 0), stop=(j == J4 - 1))
                    last.then_inc(S["y_ps"], 1)

                def turn(g, k, tail, n):
                    for j in range(J4):
                        columns(g, j)
                        if tail and j % 2:
                            output(g - 1, 1 - k, j // 2)

                turns(turn, pe)
                for r in range(GB):
                    output(NG - 1, 1, r)



def lay_out(x, ctx_2048, mask_BxS2_if0, g_xattn, g_ffn, L0_xattn_W_in, L0_xattn_b_in, L0_xattn_g_res,
            L0_xattn_g_init, L0_ffn_gate_w1, L0_ffn_gate_b1, L0_ffn_gate_w2, L0_ffn_gate_b2, L0_ffn_W1,
            L0_ffn_b1, L0_ffn_W2, L0_ffn_b2, L0_ffn_TW1, L0_ffn_Tb1, L0_ffn_TW2, L0_ffn_Tb2, L1_xattn_w_qkv,
            L1_xattn_w_proj, L1_xattn_b_proj, L1_ffn_col_emb, L1_ffn_gate_w1, L1_ffn_gate_b1, L1_ffn_gate_w2,
            L1_ffn_gate_b2, L1_ffn_W_cols, L1_ffn_b_cols, L1_ffn_proj_w, L1_ffn_proj_b, L1_ffn_ln_g,
            L1_ffn_ln_b):
    f32 = np.float32

    def rows(m):
        m = np.asarray(m)
        return m.reshape(-1, P, m.shape[-1]).transpose(1, 0, 2)

    def column(v):
        return np.asarray(v).reshape(-1, P).T

    out = {"x": x, "ctx": ctx_2048, "mask": mask_BxS2_if0, "g_xattn": g_xattn, "g_ffn": g_ffn}
    out["ident"] = np.eye(P, dtype=f32)
    out["iota"] = np.concatenate([np.tile(np.arange(T), (P, 1)), np.arange(P)[:, None]], 1).astype(f32)
    out["w_in_t"] = rows(np.asarray(L0_xattn_W_in).T)
    out["g_res_c"] = column(L0_xattn_g_res)
    out["g_init_row"] = np.asarray(L0_xattn_g_init)[:D]
    out["b_in_row"] = np.asarray(L0_xattn_b_in)[None]
    out["gate1_t"] = rows(np.asarray(L0_ffn_gate_w1).T)
    out["gate1_b"] = column(L0_ffn_gate_b1)
    gate2_t = np.asarray(L0_ffn_gate_w2).T
    out["gate2_t"] = rows(gate2_t)
    out["gate2_rep_t"] = rows(np.repeat(gate2_t, ER, 1))
    out["gate2_b"] = np.asarray(L0_ffn_gate_b2)[:, None]
    out["gate2_rep_b"] = np.repeat(np.asarray(L0_ffn_gate_b2), ER)[:, None]
    out["same_row"] = np.tile(np.eye(ER, dtype=f32), (E, 1))
    tw1 = np.asarray(L0_ffn_TW1).reshape(E, FC, P // ER, ER, D)
    out["tw1"] = tw1.transpose(1, 0, 3, 2, 4).reshape(FC, P, P // ER, D)
    tw2 = np.asarray(L0_ffn_TW2).reshape(E, D // ER, ER, FC, P)
    out["tw2"] = tw2.transpose(3, 0, 2, 1, 4).reshape(FC, P, D // ER, P)
    out["w1_t"] = np.asarray(L0_ffn_W1).T.reshape(KD, P, FC, P).transpose(2, 1, 0, 3)
    out["w2_t"] = np.asarray(L0_ffn_W2).T.reshape(FC, P, D)
    out["tb1"] = np.concatenate([np.asarray(L0_ffn_Tb1), np.asarray(L0_ffn_b1)[None]])
    out["tb2"] = np.concatenate([np.asarray(L0_ffn_Tb2), np.asarray(L0_ffn_b2)[None]])
    w_qkv = np.asarray(L1_xattn_w_qkv)
    for name, part in (("wq_t", w_qkv[:D]), ("wk_t", w_qkv[D:2 * D])):
        slots = np.zeros((D, NT, HS, SLOT), f32)
        slots[:, :, :, :DH] = part.T.reshape(D, NT, HS, DH)
        out[name] = slots.reshape(KD, P, NT, P).transpose(1, 0, 2, 3)
    out["wv_t"] = rows(w_qkv[2 * D:].T)
    out["ctx_k_t"] = np.asarray(ctx_2048)[:, :, :D].reshape(B, S2, NT, HS, DH).transpose(0, 3, 4, 2, 1)
    slots = np.zeros((NT, HS, SLOT, D), f32)
    slots[:, :, :DH] = np.asarray(L1_xattn_w_proj).T.reshape(NT, HS, DH, D)
    slots[0, 0, DH] = np.asarray(L1_xattn_b_proj)
    out["w_proj_t"] = slots.reshape(NT, P, D).transpose(1, 0, 2)
    aug = np.zeros((P, 1 + 2 * HS), f32)
    aug[DH::SLOT, 0] = 1
    for s in range(HS):
        aug[s * SLOT + DH, 1 + s] = 1
        aug[s * SLOT:(s + 1) * SLOT, 1 + HS + s] = 1
    out["shift_rows"] = aug
    out["col_emb"] = L1_ffn_col_emb
    out["cgate1"] = rows(L1_ffn_gate_w1)
    out["cgate1_b"] = column(L1_ffn_gate_b1)
    out["cgate2"] = L1_ffn_gate_w2
    out["cgate2_b"] = L1_ffn_gate_b2
    out["w_cols"] = rows(np.asarray(L1_ffn_W_cols).transpose(1, 0, 2).reshape(D, F4))
    out["b_cols"] = column(np.asarray(L1_ffn_b_cols).reshape(-1))
    out["proj"] = rows(L1_ffn_proj_w)
    out["proj_b"] = L1_ffn_proj_b
    out["ln_g"] = L1_ffn_ln_g
    out["ln_b"] = L1_ffn_ln_b
    out["col_of"] = np.tile(np.repeat(np.eye(C4, dtype=f32), N4, 1), (3, 1))
    out["col_less"] = np.tile(np.arange(C4) - float(C4), (P, 1)).astype(f32)
    return {k: np.ascontiguousarray(v) for k, v in out.items()}


def kernel(**inputs):
    import concourse.bacc as bacc
    from concourse.bass_utils import run_bass_kernel_spmd

    nc = bacc.Bacc("TRN2", target_bir_lowering=False, num_devices=1)
    arrays = {f"in_{k}": v for k, v in lay_out(**inputs).items()}
    a = {k[3:]: nc.dram_tensor(k, v.shape, mybir.dt.from_np(v.dtype), kind="ExternalInput").ap()
         for k, v in arrays.items()}
    out = nc.dram_tensor("out_x", (B, T, D), F32, kind="ExternalOutput").ap()
    build(nc, a, out)
    return run_bass_kernel_spmd(nc, [arrays], core_ids=[0]).results[0]["out_x"]
```
